# Optimizing a Trainium2 kernel written in Bass

```python
import numpy as np
import jax
import jax.numpy as jnp

def _softmax(x, axis=-1):
    return jax.nn.softmax(x, axis=axis)

def _gelu(x):
    return jax.nn.gelu(x, approximate=True)

def _silu(x):
    return jax.nn.silu(x)

def _sigmoid(x):
    return jax.nn.sigmoid(x)

def _layernorm(x, axis=-1, eps=1e-05):
    m = jnp.mean(x, axis=axis, keepdims=True)
    v = jnp.var(x, axis=axis, keepdims=True)
    return (x - m) / jnp.sqrt(v + eps)

def _scatter_add(tgt, idx, src, axis=0):
    return tgt.at[idx].add(src)

def _segment_sum(src, seg, n):
    return jax.ops.segment_sum(src, seg, n)
kernel_name = 'mk_prb_d2_jaxref_r8_443dd4'

def setup_inputs(seed: int=0):
    np.random.seed(seed)
    _w = jnp.asarray

    def _L0_attn_setup():
        import jax, jax.numpy as jnp
        import numpy as np
        BATCH, SEQ, D_EMBED, N_HEADS, D_HEAD = (1, 256, 128, 16, 64)
        MASK_VAL = 10000000000.0
        key = jax.random.key(seed)
        ks = jax.random.split(key, 5)
        s = 1.0 / np.sqrt(D_EMBED).astype(np.float32)
        return {'x': jax.random.normal(ks[0], (BATCH, SEQ, D_EMBED), jnp.float32), 'W_Q': jax.random.normal(ks[1], (N_HEADS, D_HEAD, D_EMBED), jnp.float32) * s, 'W_K': jax.random.normal(ks[2], (N_HEADS, D_HEAD, D_EMBED), jnp.float32) * s, 'W_V': jax.random.normal(ks[3], (N_HEADS, D_HEAD, D_EMBED), jnp.float32) * s, 'W_O': jax.random.normal(ks[4], (N_HEADS, D_EMBED, D_HEAD), jnp.float32) * s}
    _L0_attn_in = _L0_attn_setup()

    def _L0_ffn_setup():
        import jax, jax.numpy as jnp
        import numpy as np
        FP8_MAX = 448.0
        SCALE = 1.0
        _FP8_DTYPE = getattr(jnp, 'float8_e4m3fn', jnp.float16)

        def quantize_e4m3(t, scale):
            return jnp.clip(t / scale, -FP8_MAX, FP8_MAX).astype(_FP8_DTYPE)
        key = jax.random.key(seed)
        kx, kw = jax.random.split(key)
        B, N, C, F = (8, 512, 128, 128)
        x = jax.random.normal(kx, (B, N, C), dtype=jnp.float32)
        weight = jax.random.normal(kw, (F, C), dtype=jnp.float32) * 0.02
        bias = jnp.zeros((F,), dtype=jnp.float32)
        return {'x': x, 'weight': weight, 'bias': bias}
    _L0_ffn_in = _L0_ffn_setup()

    def _L1_attn_setup():
        import jax, jax.numpy as jnp
        import numpy as np
        import math
        NUM_HEADS = 16

        def rotate_half(x):
            x1 = x[..., ::2]
            x2 = x[..., 1::2]
            return jnp.concatenate((-x2, x1), axis=-1)

        def rotary_tables(seq_len, head_dim, dtype):
            inv_freq = 1.0 / 10000.0 ** (jnp.arange(0, head_dim, 2, dtype=jnp.float32) / head_dim)
            t = jnp.arange(seq_len, dtype=jnp.float32)
            freqs = t[:, None] * inv_freq[None, :]
            emb = jnp.concatenate((freqs, freqs), axis=-1)
            cos = jnp.cos(emb)[None, None, :, :].astype(dtype)
            sin = jnp.sin(emb)[None, None, :, :].astype(dtype)
            return (cos, sin)
        key = jax.random.key(seed)
        k1, k2, k3, k4 = jax.random.split(key, 4)
        B, T, D = (2, 256, 128)
        scale = 1.0 / math.sqrt(D)
        x = jax.random.normal(k1, (B, T, D), dtype=jnp.float32)
        w_qkv = jax.random.normal(k2, (3 * D, D), dtype=jnp.float32) * scale
        w_out = jax.random.normal(k3, (D, D), dtype=jnp.float32) * scale
        b_out = jax.random.normal(k4, (D,), dtype=jnp.float32) * scale
        return {'x': x, 'w_qkv': w_qkv, 'w_out': w_out, 'b_out': b_out}
    _L1_attn_in = _L1_attn_setup()

    def _L1_ffn_setup():
        import jax, jax.numpy as jnp
        import numpy as np
        DIM = 128
        DEPTH = 6
        HEADS = 16
        DIM_HEAD = 64
        WINDOW = 32
        INNER = HEADS * DIM_HEAD
        DIM_INNER = int(DIM * 4 * 2 / 3)
        QK_SCALE = 8.0

        def shift_tokens(t):
            a, s = jnp.split(t, 2, -1)
            s = jnp.pad(s, ((0, 0), (1, 0), (0, 0)))[:, :-1]
            return jnp.concatenate([a, s], -1)

        def l2norm(t):
            return t / jnp.maximum(jnp.linalg.norm(t, axis=-1, keepdims=True), 1e-12)

        def rotate_half(x):
            x1, x2 = jnp.split(x, 2, -1)
            return jnp.concatenate([-x2, x1], -1)

        def rotary_tables(n):
            half = jnp.arange(0, DIM_HEAD, 2, dtype=jnp.float32)
            inv_freq = 1.0 / 10000.0 ** (half / DIM_HEAD)
            t = jnp.arange(n, dtype=jnp.float32)
            freqs = t[:, None] * inv_freq[None, :]
            freqs = jnp.concatenate([freqs, freqs], -1)
            base_scale = (half + 0.4 * DIM_HEAD) / (1.4 * DIM_HEAD)
            power = (t - n // 2) / (WINDOW // 2)
            scale = base_scale[None, :] ** power[:, None]
            scale = jnp.concatenate([scale, scale], -1)
            return (freqs, scale)

        def local_attention(q, k, v):
            b, h, n, d = q.shape
            w = WINDOW
            nw = n // w
            bq = q.reshape(b, h, nw, w, d)
            bk = k.reshape(b, h, nw, w, d)
            bv = v.reshape(b, h, nw, w, d)

            def look(t):
                p = jnp.pad(t, ((0, 0), (0, 0), (1, 0), (0, 0), (0, 0)))
                return jnp.concatenate([p[:, :, :nw], p[:, :, 1:]], axis=3)
            bk2, bv2 = (look(bk), look(bv))
            seq = jnp.arange(n).reshape(nw, w)
            seq_p = jnp.pad(seq, ((1, 0), (0, 0)), constant_values=-1)
            jt = jnp.concatenate([seq_p[:nw], seq_p[1:]], axis=1)
            it = seq[:, :, None]
            jb = jt[:, None, :]
            mask = (it < jb) | (it > jb + w) | (jb == -1)
            sim = jnp.einsum('bhwie,bhwje->bhwij', bq, bk2) * QK_SCALE
            sim = jnp.where(mask, -jnp.finfo(sim.dtype).max, sim)
            attn = jax.nn.softmax(sim, -1)
            out = jnp.einsum('bhwij,bhwje->bhwie', attn, bv2)
            return out.reshape(b, h, n, d)

        def attn_layer(x, Wqkv, qs, ksc, Wo):
            b, n, _ = x.shape
            qkv = x @ Wqkv
            q, k, v = jnp.split(qkv, 3, -1)
            sh = lambda t: t.reshape(b, n, HEADS, DIM_HEAD).transpose(0, 2, 1, 3)
            q, k, v = (sh(q), sh(k), sh(v))
            q = l2norm(q) * qs
            k = l2norm(k) * ksc
            freqs, scale = rotary_tables(n)
            cos, sin = (jnp.cos(freqs), jnp.sin(freqs))
            q = q * cos * scale + rotate_half(q) * sin * scale
            inv = 1.0 / scale
            k = k * cos * inv + rotate_half(k) * sin * inv
            out = local_attention(q, k, v)
            out = out.transpose(0, 2, 1, 3).reshape(b, n, INNER)
            return out @ Wo

        def ffn_layer(x, g, bln, W1, b1, W2, b2):
            mu = x.mean(-1, keepdims=True)
            var = ((x - mu) ** 2).mean(-1, keepdims=True)
            xn = (x - mu) / jnp.sqrt(var + 1e-05) * g + bln
            hg = xn @ W1 + b1
            a, gate = jnp.split(hg, 2, -1)
            return a * jax.nn.gelu(gate, approximate=False) @ W2 + b2
        key = jax.random.key(seed)
        ks = jax.random.split(key, 8)
        B, N = (2, 256)
        init = lambda k, shape: jax.random.normal(k, shape, jnp.float32) * 0.02
        return {'x': jax.random.normal(ks[0], (B, N, DIM), jnp.float32), 'Wqkv': init(ks[1], (DEPTH, DIM, 3 * INNER)), 'q_scale': jnp.ones((DEPTH, DIM_HEAD), jnp.float32), 'k_scale': jnp.ones((DEPTH, DIM_HEAD), jnp.float32), 'Wo': init(ks[2], (DEPTH, INNER, DIM)), 'ln_g': jnp.ones((DEPTH, DIM), jnp.float32), 'ln_b': jnp.zeros((DEPTH, DIM), jnp.float32), 'W1': init(ks[3], (DEPTH, DIM, 2 * DIM_INNER)), 'b1': jnp.zeros((DEPTH, 2 * DIM_INNER), jnp.float32), 'W2': init(ks[4], (DEPTH, DIM_INNER, DIM)), 'b2': jnp.zeros((DEPTH, DIM), jnp.float32)}
    _L1_ffn_in = _L1_ffn_setup()
    _d = {'L0_attn_x': _L0_attn_in['x'], 'L0_attn_W_Q': _L0_attn_in['W_Q'], 'L0_attn_W_K': _L0_attn_in['W_K'], 'L0_attn_W_V': _L0_attn_in['W_V'], 'L0_attn_W_O': _L0_attn_in['W_O'], 'L0_ffn_weight': _L0_ffn_in['weight'], 'L0_ffn_bias': _L0_ffn_in['bias'], 'L1_attn_w_qkv': _L1_attn_in['w_qkv'], 'L1_attn_w_out': _L1_attn_in['w_out'], 'L1_attn_b_out': _L1_attn_in['b_out'], 'L1_ffn_Wqkv': _L1_ffn_in['Wqkv'], 'L1_ffn_q_scale': _L1_ffn_in['q_scale'], 'L1_ffn_k_scale': _L1_ffn_in['k_scale'], 'L1_ffn_Wo': _L1_ffn_in['Wo'], 'L1_ffn_ln_g': _L1_ffn_in['ln_g'], 'L1_ffn_ln_b': _L1_ffn_in['ln_b'], 'L1_ffn_W1': _L1_ffn_in['W1'], 'L1_ffn_b1': _L1_ffn_in['b1'], 'L1_ffn_W2': _L1_ffn_in['W2'], 'L1_ffn_b2': _L1_ffn_in['b2']}
    _x0 = _d['L0_attn_x']
    _d['L0_attn_x'] = jax.random.normal(jax.random.fold_in(jax.random.key(seed), 1), (4, 1024, 128), dtype=_x0.dtype)
    del _x0
    return _d

def reference(L0_attn_x, L0_attn_W_Q, L0_attn_W_K, L0_attn_W_V, L0_attn_W_O, L0_ffn_weight, L0_ffn_bias, L1_attn_w_qkv, L1_attn_w_out, L1_attn_b_out, L1_ffn_Wqkv, L1_ffn_q_scale, L1_ffn_k_scale, L1_ffn_Wo, L1_ffn_ln_g, L1_ffn_ln_b, L1_ffn_W1, L1_ffn_b1, L1_ffn_W2, L1_ffn_b2):

    def _L0_attn_ref(x, W_Q, W_K, W_V, W_O):
        import jax, jax.numpy as jnp
        import numpy as np
        BATCH, SEQ, D_EMBED, N_HEADS, D_HEAD = (1, 256, 128, 16, 64)
        MASK_VAL = 10000000000.0
        q = jnp.einsum('ahe,bce->bach', W_Q, x)
        k = jnp.einsum('ahe,bce->bach', W_K, x)
        v = jnp.einsum('ahe,bce->bach', W_V, x)
        n = x.shape[1]
        scores = jnp.einsum('bach,baCh->bacC', k, q)
        causal = jnp.tril(jnp.ones((n, n), dtype=bool))
        masked = jnp.where(causal, scores, jnp.float32(-MASK_VAL))
        attn = jax.nn.softmax(masked / np.float32(np.sqrt(D_HEAD)), axis=-1)
        z = jnp.einsum('bacC,baCh->bach', attn, v)
        out = jnp.einsum('aeh,bach->bce', W_O, z)
        return out

    def _L0_ffn_ref(x, weight, bias):
        import jax, jax.numpy as jnp
        import numpy as np
        FP8_MAX = 448.0
        SCALE = 1.0
        _FP8_DTYPE = getattr(jnp, 'float8_e4m3fn', jnp.float16)

        def quantize_e4m3(t, scale):
            return jnp.clip(t / scale, -FP8_MAX, FP8_MAX).astype(_FP8_DTYPE)
        B, N, C = x.shape
        x2d = x.reshape(B * N, C)
        x_mat = quantize_e4m3(x2d, SCALE).astype(jnp.float16)
        w_mat = quantize_e4m3(weight, SCALE).astype(jnp.float16)
        out2d = (x_mat @ w_mat.T).astype(jnp.float32) * (SCALE * SCALE)
        out2d = out2d + bias
        return out2d.reshape(B, N, -1)

    def _L1_attn_ref(x, w_qkv, w_out, b_out):
        import jax, jax.numpy as jnp
        import numpy as np
        import math
        NUM_HEADS = 16

        def rotate_half(x):
            x1 = x[..., ::2]
            x2 = x[..., 1::2]
            return jnp.concatenate((-x2, x1), axis=-1)

        def rotary_tables(seq_len, head_dim, dtype):
            inv_freq = 1.0 / 10000.0 ** (jnp.arange(0, head_dim, 2, dtype=jnp.float32) / head_dim)
            t = jnp.arange(seq_len, dtype=jnp.float32)
            freqs = t[:, None] * inv_freq[None, :]
            emb = jnp.concatenate((freqs, freqs), axis=-1)
            cos = jnp.cos(emb)[None, None, :, :].astype(dtype)
            sin = jnp.sin(emb)[None, None, :, :].astype(dtype)
            return (cos, sin)
        B, T, D = x.shape
        H = NUM_HEADS
        hd = D // H
        qkv = x @ w_qkv.T
        q, k, v = jnp.split(qkv, 3, axis=-1)

        def to_heads(a):
            return a.reshape(B, T, H, hd).transpose(0, 2, 1, 3)
        q, k, v = (to_heads(q), to_heads(k), to_heads(v))
        cos, sin = rotary_tables(T, hd, x.dtype)
        q = q * cos + rotate_half(q) * sin
        k = k * cos + rotate_half(k) * sin
        attn = jnp.einsum('bhqd,bhkd->bhqk', q, k) / math.sqrt(hd)
        attn = jax.nn.softmax(attn, axis=-1)
        out = jnp.einsum('bhqk,bhkd->bhqd', attn, v)
        out = out.transpose(0, 2, 1, 3).reshape(B, T, D)
        return out @ w_out.T + b_out

    def _L1_ffn_ref(x, Wqkv, q_scale, k_scale, Wo, ln_g, ln_b, W1, b1, W2, b2):
        import jax, jax.numpy as jnp
        import numpy as np
        DIM = 128
        DEPTH = 6
        HEADS = 16
        DIM_HEAD = 64
        WINDOW = 32
        INNER = HEADS * DIM_HEAD
        DIM_INNER = int(DIM * 4 * 2 / 3)
        QK_SCALE = 8.0

        def shift_tokens(t):
            a, s = jnp.split(t, 2, -1)
            s = jnp.pad(s, ((0, 0), (1, 0), (0, 0)))[:, :-1]
            return jnp.concatenate([a, s], -1)

        def l2norm(t):
            return t / jnp.maximum(jnp.linalg.norm(t, axis=-1, keepdims=True), 1e-12)

        def rotate_half(x):
            x1, x2 = jnp.split(x, 2, -1)
            return jnp.concatenate([-x2, x1], -1)

        def rotary_tables(n):
            half = jnp.arange(0, DIM_HEAD, 2, dtype=jnp.float32)
            inv_freq = 1.0 / 10000.0 ** (half / DIM_HEAD)
            t = jnp.arange(n, dtype=jnp.float32)
            freqs = t[:, None] * inv_freq[None, :]
            freqs = jnp.concatenate([freqs, freqs], -1)
            base_scale = (half + 0.4 * DIM_HEAD) / (1.4 * DIM_HEAD)
            power = (t - n // 2) / (WINDOW // 2)
            scale = base_scale[None, :] ** power[:, None]
            scale = jnp.concatenate([scale, scale], -1)
            return (freqs, scale)

        def local_attention(q, k, v):
            b, h, n, d = q.shape
            w = WINDOW
            nw = n // w
            bq = q.reshape(b, h, nw, w, d)
            bk = k.reshape(b, h, nw, w, d)
            bv = v.reshape(b, h, nw, w, d)

            def look(t):
                p = jnp.pad(t, ((0, 0), (0, 0), (1, 0), (0, 0), (0, 0)))
                return jnp.concatenate([p[:, :, :nw], p[:, :, 1:]], axis=3)
            bk2, bv2 = (look(bk), look(bv))
            seq = jnp.arange(n).reshape(nw, w)
            seq_p = jnp.pad(seq, ((1, 0), (0, 0)), constant_values=-1)
            jt = jnp.concatenate([seq_p[:nw], seq_p[1:]], axis=1)
            it = seq[:, :, None]
            jb = jt[:, None, :]
            mask = (it < jb) | (it > jb + w) | (jb == -1)
            sim = jnp.einsum('bhwie,bhwje->bhwij', bq, bk2) * QK_SCALE
            sim = jnp.where(mask, -jnp.finfo(sim.dtype).max, sim)
            attn = jax.nn.softmax(sim, -1)
            out = jnp.einsum('bhwij,bhwje->bhwie', attn, bv2)
            return out.reshape(b, h, n, d)

        def attn_layer(x, Wqkv, qs, ksc, Wo):
            b, n, _ = x.shape
            qkv = x @ Wqkv
            q, k, v = jnp.split(qkv, 3, -1)
            sh = lambda t: t.reshape(b, n, HEADS, DIM_HEAD).transpose(0, 2, 1, 3)
            q, k, v = (sh(q), sh(k), sh(v))
            q = l2norm(q) * qs
            k = l2norm(k) * ksc
            freqs, scale = rotary_tables(n)
            cos, sin = (jnp.cos(freqs), jnp.sin(freqs))
            q = q * cos * scale + rotate_half(q) * sin * scale
            inv = 1.0 / scale
            k = k * cos * inv + rotate_half(k) * sin * inv
            out = local_attention(q, k, v)
            out = out.transpose(0, 2, 1, 3).reshape(b, n, INNER)
            return out @ Wo

        def ffn_layer(x, g, bln, W1, b1, W2, b2):
            mu = x.mean(-1, keepdims=True)
            var = ((x - mu) ** 2).mean(-1, keepdims=True)
            xn = (x - mu) / jnp.sqrt(var + 1e-05) * g + bln
            hg = xn @ W1 + b1
            a, gate = jnp.split(hg, 2, -1)
            return a * jax.nn.gelu(gate, approximate=False) @ W2 + b2
        for i in range(DEPTH):
            x = attn_layer(shift_tokens(x), Wqkv[i], q_scale[i], k_scale[i], Wo[i]) + x
            x = ffn_layer(shift_tokens(x), ln_g[i], ln_b[i], W1[i], b1[i], W2[i], b2[i]) + x
        return x
    x = L0_attn_x
    xn = _layernorm(x, axis=-1)
    x = x + _L0_attn_ref(xn, L0_attn_W_Q, L0_attn_W_K, L0_attn_W_V, L0_attn_W_O) + _L0_ffn_ref(xn, L0_ffn_weight, L0_ffn_bias)
    xn = _layernorm(x, axis=-1)
    x = x + _L1_attn_ref(xn, L1_attn_w_qkv, L1_attn_w_out, L1_attn_b_out) + _L1_ffn_ref(xn, L1_ffn_Wqkv, L1_ffn_q_scale, L1_ffn_k_scale, L1_ffn_Wo, L1_ffn_ln_g, L1_ffn_ln_b, L1_ffn_W1, L1_ffn_b1, L1_ffn_W2, L1_ffn_b2)
    return x

_drawn_inputs = setup_inputs


def setup_inputs(seed=0):
    import zlib

    import numpy as np

    out = dict(_drawn_inputs(seed))
    spreads = {'L0_ffn_bias': (0.0, 0.1),
     'L1_ffn_q_scale': (1.0, 0.6),
     'L1_ffn_k_scale': (1.0, 0.6),
     'L1_ffn_ln_g': (1.0, 0.6),
     'L1_ffn_ln_b': (0.0, 0.8),
     'L1_ffn_b1': (0.0, 0.8),
     'L1_ffn_b2': (0.0, 0.1)}
    factors = {'L1_ffn_W1': 3.877, 'L1_ffn_W2': 3.806, 'L1_attn_b_out': 4.523}
    for name, (base, spread) in spreads.items():
        noise = np.random.default_rng([zlib.crc32(name.encode()), seed]).standard_normal(out[name].shape)
        drawn = base * np.exp(spread * noise) if base else spread * noise
        out[name] = jnp.asarray(drawn.astype(out[name].dtype))
    for name, factor in factors.items():
        out[name] = (out[name] * factor).astype(out[name].dtype)
    return out
```

```python
from contextlib import ExitStack

import concourse.bass as bass
from concourse import mybir

F32 = mybir.dt.float32
BF16 = mybir.dt.bfloat16
F16 = mybir.dt.float16
FP8 = mybir.dt.float8e4
ALU = mybir.AluOpType
ACT = mybir.ActivationFunctionType
AX = mybir.AxisListType

P = 128
BATCH, SEQ, DIM = 4, 1024, 128
TILES = SEQ // P
ALL_TILES = BATCH * TILES
HEADS = 16
PAIRS = HEADS // 2
LN_EPS = 1e-5

L0_HD = 64
L1_HD = DIM // HEADS
SPLIT = 3
L0_MASK = -1e10

DEPTH = 6
LOC_HD = 64
WINDOW = 32
INNER = HEADS * LOC_HD
DIM_INNER = int(DIM * 4 * 2 / 3)
QK_SCALE = 8.0
LOC_KEYS = WINDOW + P
GROUP = 4
GROUPS = HEADS // GROUP
VW = LOC_HD + 1


class Mem:

    def __init__(self, nc, ctx):
        self.nc, self.ctx = nc, ctx

    def sb(self, name, shape, dt=F32):
        return self.ctx.enter_context(self.nc.sbuf_tensor(name, shape, dt))

    def ps(self, name, shape, dt=F32):
        return self.ctx.enter_context(self.nc.psum_tensor(name, shape, dt))

    def sem(self, name):
        return self.ctx.enter_context(self.nc.semaphore(name))


def load_phase(nc, keep, dram):
    with ExitStack() as ctx:
        m = Mem(nc, ctx)
        w = m.sb("w8_raw", [P, P])
        small = m.sb("w8_small", [P, P])
        large = m.sb("w8_large", [P, P])
        small8 = m.sb("w8_small8", [P, P], FP8)
        large8 = m.sb("w8_large8", [P, P], FP8)
        small_r = m.sb("w8_small_r", [P, P])
        large_r = m.sb("w8_large_r", [P, P])
        mag = m.sb("w8_mag", [P, P])
        is_large = m.sb("w8_is_large", [P, P])
        is_small = m.sb("w8_is_small", [P, P])
        loaded = m.sem("loaded")
        step = m.sem("w8_step")
        zeroed = m.sem("zeroed")
        with nc.Block() as block:

            @block.sync
            def _(sp):
                sp.dma_start(keep.xres[:], dram["x"].rearrange("(t p) c -> p t c", p=P)).then_inc(loaded, 16)
                sp.dma_start(w[:], dram["w8T"]).then_inc(loaded, 16)
                sp.dma_start(keep.ident[:], dram["ident"]).then_inc(loaded, 16)
                sp.dma_start(keep.bias0[:], dram["bias0"].rearrange("(a c) -> a c", a=1).broadcast_to([P, P])).then_inc(loaded, 16)
                sp.dma_start(keep.bias1[:], dram["b_out"].rearrange("(a c) -> a c", a=1).broadcast_to([P, P])).then_inc(loaded, 16)
                sp.wait_ge(loaded, 80)

            @block.gpsimd
            def _(pool):
                pool.memset(keep.y_in[:], 0.0).then_inc(zeroed, 1)
                pool.memset(keep.y_mid[:], 0.0).then_inc(zeroed, 1)
                pool.memset(keep.neg_half[:], -0.5).then_inc(zeroed, 1)
                pool.wait_ge(zeroed, 3)

            @block.vector
            def _(dve):
                dve.wait_ge(loaded, 80)
                dve.tensor_copy(keep.identb[:], keep.ident[:]).then_inc(step, 1)
                dve.tensor_scalar(small[:], w[:], 128.0, -128.0, ALU.min, ALU.max).then_inc(step, 1)
                dve.tensor_scalar(large[:], w[:], 448.0, -448.0, ALU.min, ALU.max).then_inc(step, 1)
                dve.wait_ge(step, 3)
                dve.tensor_copy(small8[:], small[:], saturate=False).then_inc(step, 1)
                dve.tensor_scalar(large8[:], large[:], 0.5, None, ALU.mult, saturate=False).then_inc(step, 1)
                dve.tensor_scalar(mag[:], large[:], -1.0, None, ALU.mult).then_inc(step, 1)
                dve.wait_ge(step, 6)
                dve.tensor_tensor(is_small[:], mag[:], large[:], ALU.max).then_inc(step, 1)
                dve.wait_ge(step, 7)
                dve.tensor_scalar(is_large[:], is_small[:], 128.0, 2.0, ALU.is_gt, ALU.mult).then_inc(step, 1)
                dve.wait_ge(step, 8)
                dve.tensor_scalar(is_small[:], is_large[:], -0.5, 1.0, ALU.mult, ALU.add).then_inc(step, 1)
                dve.wait_ge(step, 9)
                dve.tensor_tensor(small_r[:], small8[:], is_small[:], ALU.mult).then_inc(step, 1)
                dve.tensor_tensor(large_r[:], large8[:], is_large[:], ALU.mult).then_inc(step, 1)
                dve.wait_ge(step, 11)
                dve.tensor_tensor(keep.w8[:], small_r[:], large_r[:], ALU.add).then_inc(step, 1)
                dve.wait_ge(step, 12)


NT = 4
NORM_STEPS = ALL_TILES // NT


def norm0_phase(nc, keep):
    with ExitStack() as ctx:
        m = Mem(nc, ctx)
        stats = m.sb("n0_stats", [P, NT, 6])
        meanvar = m.sb("n0_meanvar", [P, NT, 2])
        var = m.sb("n0_var", [P, NT])
        rstd = m.sb("n0_rstd", [P, NT])
        xn = m.sb("n0_xn", [P, NT, P])
        x8 = m.sb("n0_x8", [P, NT * P], FP8)
        x8b = m.sb("n0_x8b", [P, NT * P], BF16)
        y16 = m.sb("n0_y16", [P, NT, P], F16)
        xbias = m.sb("n0_xbias", [P, NT, P])
        ps_t = m.ps("n0_ps_t", [P, NT * P])
        ps_y = m.ps("n0_ps_y", [P, NT, P])
        stats_done, var_done, rstd_done = m.sem("n0_stats_done"), m.sem("n0_var_done"), m.sem("n0_rstd_done")
        var_eps = m.sem("n0_var_eps")
        xn_done, transposed, xnT_done = m.sem("n0_xn_done"), m.sem("n0_transposed"), m.sem("n0_xnT_done")
        x8_done, x8b_done, mm_done, y16_done = m.sem("n0_x8_done"), m.sem("n0_x8b_done"), m.sem("n0_mm_done"), m.sem("n0_y16_done")
        bias_done, x_done = m.sem("n0_bias_done"), m.sem("n0_x_done")
        with nc.Block() as block:

            @block.vector
            def _(dve):
                dve.sem_inc(y16_done, 1)
                with dve.Fori(0, NORM_STEPS) as g:
                    for j in range(NT):
                        dve.bn_stats(stats[:, j, :], keep.xres[:, bass.ds(g * NT + j, 1), :].rearrange("p a c -> p (a c)")).then_inc(stats_done, 1)
                    dve.wait_ge(stats_done, g * NT + NT)
                    dve.nop(nofuse=True)
                    for j in range(NT):
                        dve.bn_aggr(meanvar[:, j, :], stats[:, j, :]).then_inc(var_done, 1)
                    dve.wait_ge(rstd_done, g + 1)
                    for j in range(NT):
                        dve.tensor_scalar(xn[:, j, :], keep.xres[:, bass.ds(g * NT + j, 1), :].rearrange("p a c -> p (a c)"),
                                          meanvar[:, j, 0:1], rstd[:, j:j + 1], ALU.subtract, ALU.mult).then_inc(xn_done, 1)
                    dve.wait_ge(xnT_done, g + 1)
                    dve.nop(nofuse=True)
                    dve.tensor_copy(x8[:], ps_t[:], saturate=False).then_inc(x8_done, 1)
                    dve.wait_ge(x8_done, g + 1)
                    dve.nop(nofuse=True)
                    dve.tensor_copy(x8b[:], x8[:]).then_inc(x8b_done, 1)
                    dve.wait_ge(mm_done, g + 1)
                    dve.tensor_copy(y16[:], ps_y[:]).then_inc(y16_done, 1)
                    dve.wait_ge(y16_done, g + 2)
                    dve.wait_ge(bias_done, g + 1)
                    dve.tensor_tensor(keep.xres[:, bass.ds(g * NT, NT), :], y16[:], xbias[:], ALU.add).then_inc(x_done, 1)

            @block.gpsimd
            def _(pool):
                with pool.Fori(0, NORM_STEPS) as g:
                    pool.wait_ge(var_done, g * NT + NT)
                    pool.nop(nofuse=True)
                    pool.tensor_scalar(var[:], meanvar[:, :, 1], LN_EPS, None, ALU.add).then_inc(var_eps, 1)
                    pool.wait_ge(var_eps, g + 1)
                    pool.tensor_tensor(rstd[:], var[:], keep.neg_half[:, 0:NT], ALU.pow).then_inc(rstd_done, 1)
                    pool.tensor_tensor(xbias[:], keep.xres[:, bass.ds(g * NT, NT), :],
                                       keep.bias0[:].rearrange("p (a c) -> p a c", a=1).broadcast_to([P, NT, P]), ALU.add).then_inc(bias_done, 1)
                    pool.wait_ge(x_done, g + 1)

            @block.tensor
            def _(pe):
                with pe.Fori(0, NORM_STEPS) as g:
                    pe.wait_ge(xn_done, g * NT + NT)
                    for j in range(NT):
                        last = pe.transpose(ps_t[:, j * P:(j + 1) * P], xn[:, j, :], keep.ident[:])
                    last.then_inc(transposed, 1)
                    pe.wait_ge(x8b_done, g + 1)
                    pe.wait_ge(y16_done, g + 1)
                    for j in range(NT):
                        last = pe.matmul(ps_y[:, j, :], x8b[:, j * P:(j + 1) * P], keep.w8[:], start=True, stop=True)
                    last.then_inc(mm_done, 1)

            @block.scalar
            def _(act):
                with act.Fori(0, NORM_STEPS) as g:
                    act.wait_ge(transposed, g + 1)
                    act.copy(keep.xnT[:, bass.ds(g * NT * P, NT * P)], ps_t[:]).then_inc(xnT_done, 1)


def attention_phase(nc, keep, which):
    l0 = which == 0
    a = f"a{which}_"
    vd = L0_HD if l0 else L1_HD
    odt = F32 if l0 else BF16
    scale = 1.0 / float(vd) ** 0.5
    width = HEADS * vd
    chunks = width // P
    UNITS = 4 * TILES
    PREP = 6 if l0 else 2
    units = [(pl, h, t) for pl in range(2) for h in range(2) for t in range(TILES)]
    blocks = [(t + 1 if l0 else TILES) for _, _, t in units]
    second = [n > 4 for n in blocks]
    n_second = sum(second)
    second_at = [sum(second[:u]) for u in range(UNITS)]
    prep_at = {16 * pl + 5 + (c if l0 else 4 * c): (pl, c) for pl in range(2) for c in range(PREP)}

    with ExitStack() as ctx:
        m = Mem(nc, ctx)
        rowT = [m.sb(f"{a}rowT{s}", [P, SEQ], odt) for s in range(2)]
        colT = [m.sb(f"{a}colT{s}", [P, SEQ], odt) for s in range(2)]
        val = [m.sb(f"{a}val{s}", [P, TILES, 2 * vd]) for s in range(2)]
        prob = m.sb(f"{a}prob", [P, 2, SEQ])
        probT = m.sb(f"{a}probT", [P, 2, TILES, P])
        neg_max = m.sb(f"{a}neg_max", [P, 4])
        row_max = m.sb(f"{a}row_max", [P, 4])
        den = m.sb(f"{a}den", [P, 4])
        rden = m.sb(f"{a}rden", [P, 4])
        zn = m.sb(f"{a}zn", [P, TILES, width])
        if l0:
            wqkv = m.sb(f"{a}wqkv", [P, 3, width])
            wstage = m.sb(f"{a}wstage", [P, 3, P])
            xstage = m.sb(f"{a}xstage", [P, SEQ])
            wout = m.sb(f"{a}wout", [P, chunks, P])
            mask = m.sb(f"{a}mask", [P, P], BF16)
        else:
            stage = m.sb(f"{a}stage", [P, 2, TILES, 2, 64], BF16)
            wout = m.sb(f"{a}wout", [P, chunks, P])
        ps_s = m.ps(f"{a}ps_s", [P, 2, SEQ])
        ps_t = m.ps(f"{a}ps_t", [P, 2, 4, P])
        ps_z = m.ps(f"{a}ps_z", [P, 512])
        ps_m = m.ps(f"{a}ps_m", [P, 512])
        w_loaded, mask_done = m.sem(f"{a}w_loaded"), m.sem(f"{a}mask_done")
        staged, prep_mm, prep_copied = m.sem(f"{a}staged"), m.sem(f"{a}prep_mm"), m.sem(f"{a}prep_copied")
        scored, max_done, negmax_done, exp_done = (m.sem(a + x) for x in ("scored", "max_done", "negmax_done", "exp_done"))
        t_bank = [m.sem(f"{a}t_bank{k}") for k in range(2)]
        copied = [m.sem(f"{a}copied{k}") for k in range(2)]
        pv_done, rden_done, z_done = m.sem(f"{a}pv_done"), m.sem(f"{a}rden_done"), m.sem(f"{a}z_done")
        o_t = [m.sem(f"{a}o_t{k}") for k in range(2)]
        o_c = [m.sem(f"{a}o_c{k}") for k in range(2)]
        o_mm, o_add, o_bias = m.sem(f"{a}o_mm"), m.sem(f"{a}o_add"), m.sem(f"{a}o_bias")
        PER_B = 4
        halves = 2 if chunks > 4 else 1

        with nc.Block() as block:

            @block.sync
            def _(sp):
                if l0:
                    for k in range(3):
                        sp.dma_start(wqkv[:, k, :], keep.dram["l0_w"][k]).then_inc(w_loaded, 16)
                    sp.dma_start(mask[:], keep.dram["mask0"]).then_inc(w_loaded, 16)
                    sp.dma_start(wout[:], keep.dram["l0_wo"].rearrange("(k p) e -> p k e", p=P)).then_inc(w_loaded, 16)
                    sp.wait_ge(w_loaded, 80)
                else:
                    sp.dma_start(wout[:, 0, :], keep.dram["l1_wo"]).then_inc(w_loaded, 16)
                    sp.wait_ge(w_loaded, 16)

            @block.gpsimd
            def _(pool):
                if l0:
                    pool.wait_ge(w_loaded, 80)

                    def stage_pair(n1):
                        w = n1 & (PAIRS - 1)
                        b = (n1 >> 3) & (BATCH - 1)
                        pool.wait_ge(prep_mm, n1 * PREP + 1)
                        pool.nop(nofuse=True)
                        pool.tensor_copy(wstage[:], wqkv[:, :, bass.ds(w * P, P)]).then_inc(staged, 1)
                        pool.tensor_copy(xstage[:], keep.xnT[:, bass.ds(b * SEQ, SEQ)]).then_inc(staged, 1)
                else:
                    pool.memset(stage[:], 0.0).then_inc(mask_done, 1)
                    pool.wait_ge(mask_done, 1)

                    def stage_pair(n1, slot=0, first=False):
                        w = n1 & (PAIRS - 1)
                        b = (n1 >> 3) & (BATCH - 1)
                        pool.wait_ge(prep_mm, n1 * PREP + 1)
                        for side, parts in ((0, (0, 0, 1, 1, 0, 2)), (1, (0, 1, 0, 1, 2, 0))):
                            for r, part in enumerate(parts):
                                pool.tensor_copy(stage[:, side, :, :, r * L1_HD:(r + 1) * L1_HD],
                                                 keep.qk3[:, bass.ds(b * TILES, TILES), part, bass.ds(side * HEADS + w * 2, 2), :])
                        if not first:
                            pool.wait_ge(pv_done, (n1 - 1) * 2 * TILES + 2)
                        pool.nop(nofuse=True)
                        pool.tensor_copy(val[slot][:].rearrange("p t (h d) -> p t h d", h=2),
                                         keep.v1[:, bass.ds(b * TILES, TILES), bass.ds(w * 2, 2), :]).then_inc(staged, 1)

                pool.sem_inc(prep_mm, 1)
                stage_pair(0) if l0 else stage_pair(0, 0, True)
                with pool.Fori(0, BATCH * PER_B) as i:
                    for pl in range(2):
                        if l0:
                            stage_pair(2 * i + pl + 1)
                        else:
                            stage_pair(2 * i + pl + 1, (pl + 1) % 2)
                pool.wait_ge(staged, (2 if l0 else 1) * (2 * BATCH * PER_B + 1))

            @block.tensor
            def _(pe):
                def prepare(n1, c, slot):
                    pe.wait_ge(prep_copied, n1 * PREP + c + 1)
                    if l0:
                        pe.wait_ge(staged, 2 * n1 + 2)
                        if c < 4:
                            last = pe.matmul(ps_m[:], wstage[:, c // 2, :], xstage[:, (c % 2) * 512:(c % 2 + 1) * 512], start=True, stop=True)
                        else:
                            for j in range(4):
                                t = 4 * (c - 4) + j
                                last = pe.matmul(ps_m[:, j * P:(j + 1) * P], xstage[:, t * P:(t + 1) * P], wstage[:, 2, :], start=True, stop=True)
                    else:
                        pe.wait_ge(staged, n1 + 1)
                        for t in range(TILES):
                            last = pe.transpose(ps_m[:].bitcast(BF16)[:, t * P:(t + 1) * P],
                                                stage[:, c, t, :, :].rearrange("p h r -> p (h r)"), keep.identb[:])
                    last.then_inc(prep_mm, 1)

                def scores(i, u):
                    pl, h, t = units[u]
                    n = blocks[u] * P
                    if h == 0 and t == 0:
                        pe.wait_ge(prep_copied, (2 * i + pl + 1) * PREP + 1)
                    pe.wait_ge(exp_done, i * UNITS + u + 1)
                    for k in range(0, n, 512):
                        e = min(n, k + 512)
                        diag = l0 and t * P >= k and t * P < e
                        last = pe.matmul(ps_s[:, u % 2, k:e], rowT[pl][64 * h:64 * h + 64, t * P:(t + 1) * P],
                                         colT[pl][64 * h:64 * h + 64, k:e], start=True, stop=not diag)
                        if diag:
                            last = pe.matmul(ps_s[:, u % 2, t * P:(t + 1) * P], keep.identb[:], mask[:], start=False, stop=True)
                    last.then_inc(scored, 1)

                def transposes(i, u):
                    pe.wait_ge(exp_done, i * UNITS + u + 3)
                    for j in range(blocks[u]):
                        k = j // 4
                        if j == 0:
                            pe.wait_ge(copied[0], i * UNITS + u + 1)
                        if j == 4:
                            pe.wait_ge(copied[1], i * n_second + second_at[u] + 1)
                        last = pe.transpose(ps_t[:, k, j % 4, :], prob[:, u % 2, j * P:(j + 1) * P], keep.ident[:])
                        if j == 3 and blocks[u] > 4:
                            last.then_inc(t_bank[0], 1)
                    if blocks[u] <= 4:
                        last.then_inc(t_bank[0], 1)
                    else:
                        last.then_inc(t_bank[1], 1)

                def values(i, u):
                    pl, h, t = units[u]
                    pe.wait_ge(copied[0], i * UNITS + u + 2)
                    if second[u]:
                        pe.wait_ge(copied[1], i * n_second + second_at[u] + 2)
                    pe.wait_ge(z_done, i * UNITS + u + 1)
                    for j in range(blocks[u]):
                        last = pe.matmul(ps_z[:, 0:vd], probT[:, u % 2, j, :], val[pl][:, j, h * vd:(h + 1) * vd],
                                         start=(j == 0), stop=(j == blocks[u] - 1))
                    last.then_inc(pv_done, 1)

                def project(b):
                    pe.wait_ge(z_done, (b + 1) * PER_B * UNITS + 1)
                    for t in range(TILES):
                        for k in range(halves):
                            for j in range(min(4, chunks)):
                                last = pe.transpose(ps_t[:, k, j, :], zn[:, t, (4 * k + j) * P:(4 * k + j + 1) * P], keep.ident[:])
                            last.then_inc(o_t[k], 1)
                        pe.wait_ge(o_add, b * TILES + t + 1)
                        for k in range(halves):
                            pe.wait_ge(o_c[k], b * TILES + t + 1)
                            for j in range(min(4, chunks)):
                                c = 4 * k + j
                                last = pe.matmul(ps_z[:, 0:P], probT[:, 0, c, :], wout[:, c, :], start=(c == 0), stop=(c == chunks - 1))
                        last.then_inc(o_mm, 1)
                    pe.wait_ge(o_add, (b + 1) * TILES + 1)

                pe.wait_ge(w_loaded, 80 if l0 else 16)
                for c in range(PREP):
                    prepare(0, c, 0)
                with pe.Fori(0, BATCH) as b:
                    with pe.Fori(0, PER_B) as ii:
                        i = b * PER_B + ii
                        for s in range(UNITS + 3):
                            if s < UNITS:
                                scores(i, s)
                            if s in prep_at:
                                pl, c = prep_at[s]
                                prepare(2 * i + pl + 1, c, (pl + 1) % 2)
                            if 2 <= s < UNITS + 2:
                                transposes(i, s - 2)
                            if s >= 3:
                                values(i, s - 3)
                    project(b)

            @block.vector
            def _(dve):
                if l0:
                    dve.wait_ge(w_loaded, 80)
                dve.sem_inc(copied[1], 1)
                dve.sem_inc(z_done, 1)
                dve.sem_inc(o_add, 1)

                def maximum(i, u):
                    dve.wait_ge(scored, i * UNITS + u + 1)
                    dve.wait_ge(exp_done, i * UNITS + u + 1)
                    dve.tensor_reduce(row_max[:, u % 2:u % 2 + 1], ps_s[:, u % 2, 0:blocks[u] * P], AX.X, ALU.max).then_inc(max_done, 1)
                    dve.wait_ge(max_done, i * UNITS + u + 1)
                    dve.tensor_scalar(neg_max[:, u % 2:u % 2 + 1], row_max[:, u % 2:u % 2 + 1], -scale, None, ALU.mult).then_inc(negmax_done, 1)

                def copy_second(i, u):
                    dve.wait_ge(t_bank[1], i * n_second + second_at[u] + 1)
                    dve.wait_ge(pv_done, i * UNITS + u + 1)
                    dve.tensor_copy(probT[:, u % 2, 4:blocks[u], :], ps_t[:, 1, 0:blocks[u] - 4, :]).then_inc(copied[1], 1)

                def normalize(i, b, ii, u):
                    pl, h, t = units[u]
                    dve.wait_ge(pv_done, i * UNITS + u + 3)
                    dve.reciprocal(rden[:, 0:1], den[:, u % 4:u % 4 + 1]).then_inc(rden_done, 1)
                    dve.wait_ge(rden_done, i * UNITS + u + 1)
                    dve.tensor_scalar(zn[:, t, bass.ds(ii * 4 * vd + (2 * pl + h) * vd, vd)], ps_z[:, 0:vd], rden[:, 0:1], None,
                                      ALU.mult).then_inc(z_done, 1)

                def copy_values(n1, c, slot):
                    dve.wait_ge(prep_mm, n1 * PREP + c + 2)
                    dve.tensor_copy(val[slot][:, 4 * (c - 4):4 * (c - 3), :], ps_m[:].rearrange("p (t d) -> p t d", t=4)).then_inc(prep_copied, 1)

                if l0:
                    for c in (4, 5):
                        copy_values(0, c, 0)
                with dve.Fori(0, BATCH) as b:
                    with dve.Fori(0, PER_B) as ii:
                        i = b * PER_B + ii
                        for s in range(UNITS + 3):
                            if s < UNITS:
                                maximum(i, s)
                            if 2 <= s < UNITS + 2 and second[s - 2]:
                                copy_second(i, s - 2)
                            if s in prep_at and l0 and prep_at[s][1] >= 4:
                                pl, c = prep_at[s]
                                copy_values(2 * i + pl + 1, c, (pl + 1) % 2)
                            if s >= 3:
                                normalize(i, b, ii, s - 3)
                    for t in range(TILES):
                        if halves == 2:
                            dve.wait_ge(o_t[1], b * TILES + t + 1)
                            dve.wait_ge(o_add, b * TILES + t + 1)
                            dve.tensor_copy(probT[:, 0, 4:8, :], ps_t[:, 1, :, :]).then_inc(o_c[1], 1)
                        dve.wait_ge(o_mm, b * TILES + t + 1)
                        row = keep.xres[:, bass.ds(b * TILES + t, 1), :].rearrange("p a c -> p (a c)")
                        dve.tensor_tensor(row, ps_z[:, 0:P], row, ALU.add).then_inc(o_add, 1)
                    if not l0:
                        dve.wait_ge(o_add, (b + 1) * TILES + 1)
                        rows = keep.xres[:, bass.ds(b * TILES, TILES), :]
                        dve.tensor_tensor(rows, rows, keep.bias1[:].rearrange("p (a c) -> p a c", a=1).broadcast_to([P, TILES, P]),
                                          ALU.add).then_inc(o_bias, 1)

            @block.scalar
            def _(act):
                act.sem_inc(exp_done, 2)
                act.sem_inc(pv_done, 2)
                act.sem_inc(copied[0], 1)
                act.sem_inc(prep_copied, 1)

                def exponentials(i, u):
                    act.wait_ge(negmax_done, i * UNITS + u + 1)
                    act.activation(prob[:, u % 2, 0:blocks[u] * P], ps_s[:, u % 2, 0:blocks[u] * P], ACT.Exp,
                                   bias=neg_max[:, u % 2:u % 2 + 1], scale=scale, accum_out=den[:, u % 4:u % 4 + 1]).then_inc(exp_done, 1)

                def copy_first(i, u):
                    act.wait_ge(t_bank[0], i * UNITS + u + 1)
                    act.wait_ge(pv_done, i * UNITS + u + 1)
                    n = min(4, blocks[u])
                    act.copy(probT[:, u % 2, 0:n, :], ps_t[:, 0, 0:n, :]).then_inc(copied[0], 1)

                def copy_operand(n1, c, slot):
                    act.wait_ge(prep_mm, n1 * PREP + c + 2)
                    if l0:
                        dst = (rowT, colT)[c // 2][slot]
                        act.copy(dst[:, (c % 2) * 512:(c % 2 + 1) * 512], ps_m[:]).then_inc(prep_copied, 1)
                    else:
                        act.copy((rowT, colT)[c][slot][:], ps_m[:].bitcast(BF16)).then_inc(prep_copied, 1)

                for c in range(min(PREP, 4)):
                    copy_operand(0, c, 0)
                with act.Fori(0, BATCH) as b:
                    with act.Fori(0, PER_B) as ii:
                        i = b * PER_B + ii
                        for s in range(UNITS + 3):
                            if 1 <= s < UNITS + 1:
                                if s >= 3:
                                    act.wait_ge(t_bank[1] if second[s - 3] else t_bank[0],
                                                i * n_second + second_at[s - 3] + 1 if second[s - 3] else i * UNITS + s - 2)
                                exponentials(i, s - 1)
                            if 2 <= s < UNITS + 2:
                                copy_first(i, s - 2)
                            if s in prep_at and (not l0 or prep_at[s][1] < 4):
                                pl, c = prep_at[s]
                                copy_operand(2 * i + pl + 1, c, (pl + 1) % 2)
                    for t in range(TILES):
                        act.wait_ge(o_t[0], b * TILES + t + 1)
                        act.wait_ge(o_add, b * TILES + t + 1)
                        act.copy(probT[:, 0, 0:min(4, chunks), :], ps_t[:, 0, 0:min(4, chunks), :]).then_inc(o_c[0], 1)



def norm1_phase(nc, keep):
    SH = 2 * HEADS
    with ExitStack() as ctx:
        m = Mem(nc, ctx)
        stats = m.sb("n1_stats", [P, NT, 6])
        meanvar = m.sb("n1_meanvar", [P, NT, 2])
        var = m.sb("n1_var", [P, NT])
        rstd = m.sb("n1_rstd", [P, NT])
        xn = m.sb("n1_xn", [P, NT, P])
        xT = m.sb("n1_xT", [P, NT * P])
        wqkv = m.sb("n1_wqkv", [P, 3 * DIM])
        cos = m.sb("n1_cos", [P, TILES, L1_HD])
        sin = m.sb("n1_sin", [P, TILES, L1_HD])
        qk = m.sb("n1_qk", [P, NT, SH, L1_HD])
        by_cos = m.sb("n1_by_cos", [P, NT, SH, L1_HD])
        by_sin = m.sb("n1_by_sin", [P, NT, SH, L1_HD])
        rot = m.sb("n1_rot", [P, NT, SH, L1_HD])
        rest1 = m.sb("n1_rest1", [P, NT, SH, L1_HD])
        rest2 = m.sb("n1_rest2", [P, NT, SH, L1_HD])
        ps_t = m.ps("n1_ps_t", [P, NT * P])
        ps_q = m.ps("n1_ps_q", [P, NT, 512])
        loaded = m.sem("n1_loaded")
        stats_done, var_done, var_eps, rstd_done = (m.sem("n1_" + x) for x in ("stats_done", "var_done", "var_eps", "rstd_done"))
        xn_done, transposed, xT_done, mm_done = (m.sem("n1_" + x) for x in ("xn_done", "transposed", "xT_done", "mm_done"))
        qk_done, step, y_done = m.sem("n1_qk_done"), m.sem("n1_step"), m.sem("n1_y_done")
        STEPS = 9
        with nc.Block() as block:

            @block.sync
            def _(sp):
                sp.dma_start(wqkv[:], keep.dram["l1_w"]).then_inc(loaded, 16)
                sp.dma_start(cos[:], keep.dram["l1_cos"]).then_inc(loaded, 16)
                sp.dma_start(sin[:], keep.dram["l1_sin"]).then_inc(loaded, 16)
                sp.wait_ge(loaded, 48)

            @block.vector
            def _(dve):
                dve.wait_ge(loaded, 48)
                dve.sem_inc(step, 1)
                with dve.Fori(0, NORM_STEPS) as g:
                    for j in range(NT):
                        dve.bn_stats(stats[:, j, :], keep.xres[:, bass.ds(g * NT + j, 1), :].rearrange("p a c -> p (a c)")).then_inc(stats_done, 1)
                    dve.wait_ge(stats_done, g * NT + NT)
                    dve.nop(nofuse=True)
                    for j in range(NT):
                        dve.bn_aggr(meanvar[:, j, :], stats[:, j, :]).then_inc(var_done, 1)
                    dve.wait_ge(rstd_done, g + 1)
                    dve.wait_ge(y_done, g + 1)
                    for j in range(NT):
                        dve.tensor_scalar(xn[:, j, :], keep.xres[:, bass.ds(g * NT + j, 1), :].rearrange("p a c -> p (a c)"),
                                          meanvar[:, j, 0:1], rstd[:, j:j + 1], ALU.subtract, ALU.mult).then_inc(xn_done, 1)
                    half = L1_HD // 2
                    t0 = (g & 1) * NT

                    def table(tab, lo, hi):
                        return tab[:, bass.ds(t0, NT), lo:hi].rearrange("p t (a d) -> p t a d", a=1).broadcast_to([P, NT, SH, hi - lo])

                    def own(n):
                        dve.wait_ge(step, g * STEPS + n + 1)

                    dve.wait_ge(qk_done, g + 1)
                    odd_even = qk[:].rearrange("p t h (d two) -> p t h d two", two=2)
                    dve.tensor_tensor(by_cos[:], qk[:], table(cos, 0, L1_HD), ALU.mult).then_inc(step, 1)
                    dve.tensor_tensor(by_sin[:, :, :, 0:half], odd_even[:, :, :, :, 1], table(sin, 0, half), ALU.mult).then_inc(step, 1)
                    dve.tensor_tensor(by_sin[:, :, :, half:], odd_even[:, :, :, :, 0], table(sin, half, L1_HD), ALU.mult).then_inc(step, 1)
                    own(3)
                    dve.tensor_tensor(rot[:], by_cos[:], by_sin[:], ALU.add).then_inc(step, 1)
                    own(4)

                    def part(k):
                        return keep.qk3[:, bass.ds(g * NT, NT), k, :, :]

                    dve.tensor_copy(part(0), rot[:]).then_inc(step, 1)
                    own(5)
                    dve.tensor_tensor(rest1[:], rot[:], part(0), ALU.subtract).then_inc(step, 1)
                    own(6)
                    dve.tensor_copy(part(1), rest1[:]).then_inc(step, 1)
                    own(7)
                    dve.tensor_tensor(rest2[:], rest1[:], part(1), ALU.subtract).then_inc(step, 1)
                    own(8)
                    dve.tensor_copy(part(2), rest2[:]).then_inc(step, 1)

            @block.gpsimd
            def _(pool):
                pool.sem_inc(y_done, 1)
                with pool.Fori(0, NORM_STEPS) as g:
                    pool.wait_ge(var_done, g * NT + NT)
                    pool.nop(nofuse=True)
                    pool.tensor_scalar(var[:], meanvar[:, :, 1], LN_EPS, None, ALU.add).then_inc(var_eps, 1)
                    pool.wait_ge(var_eps, g + 1)
                    pool.tensor_tensor(rstd[:], var[:], keep.neg_half[:, 0:NT], ALU.pow).then_inc(rstd_done, 1)
                    pool.wait_ge(xn_done, g * NT + NT)
                    pool.nop(nofuse=True)
                    pool.tensor_copy(keep.y_in[:, bass.ds(g * NT + (g >> 1) + 1, NT), :], xn[:]).then_inc(y_done, 1)

            @block.tensor
            def _(pe):
                pe.wait_ge(loaded, 48)
                with pe.Fori(0, NORM_STEPS) as g:
                    pe.wait_ge(xn_done, g * NT + NT)
                    for j in range(NT):
                        last = pe.transpose(ps_t[:, j * P:(j + 1) * P], xn[:, j, :], keep.ident[:])
                    last.then_inc(transposed, 1)
                    pe.wait_ge(xT_done, g + 1)
                    for j in range(NT):
                        last = pe.matmul(ps_q[:, j, 0:3 * DIM], xT[:, j * P:(j + 1) * P], wqkv[:], start=True, stop=True)
                    last.then_inc(mm_done, 1)

            @block.scalar
            def _(act):
                with act.Fori(0, NORM_STEPS) as g:
                    act.wait_ge(transposed, g + 1)
                    act.copy(xT[:], ps_t[:]).then_inc(xT_done, 1)
                    act.wait_ge(mm_done, g + 1)
                    act.wait_ge(step, g * STEPS + 1)
                    act.copy(keep.v1[:, bass.ds(g * NT, NT), :, :].rearrange("p t h d -> p t (h d)"), ps_q[:, :, 2 * DIM:3 * DIM])
                    act.copy(qk[:].rearrange("p t h d -> p t (h d)"), ps_q[:, :, 0:2 * DIM]).then_inc(qk_done, 1)


class Keep:
    pass


def build(nc, dram, out):
    with ExitStack() as ctx:
        m = Mem(nc, ctx)
        keep = Keep()
        keep.dram = dram
        keep.ident = m.sb("ident", [P, P])
        keep.identb = m.sb("identb", [P, P], BF16)
        keep.neg_half = m.sb("neg_half", [P, 2 * HEADS])
        keep.y_in = m.sb("y_in", [P, BATCH * (TILES + 1) + 1, P])
        keep.y_mid = m.sb("y_mid", [P, BATCH * (TILES + 1) + 1, P])
        with ExitStack() as cx:
            mx = Mem(nc, cx)
            keep.xres = mx.sb("xres", [P, ALL_TILES, P])
            keep.bias0 = mx.sb("bias0", [P, P])
            keep.bias1 = mx.sb("bias1", [P, P])
            keep.w8 = mx.sb("w8", [P, P], BF16)
            load_phase(nc, keep, dram)
            with ExitStack() as c0:
                keep.xnT = Mem(nc, c0).sb("xnT", [P, BATCH * SEQ])
                norm0_phase(nc, keep)
                attention_phase(nc, keep, 0)
            with ExitStack() as c1:
                keep.qk3 = Mem(nc, c1).sb("qk3", [P, ALL_TILES, SPLIT, 2 * HEADS, L1_HD], BF16)
                keep.v1 = Mem(nc, c1).sb("v1", [P, ALL_TILES, HEADS, L1_HD])
                norm1_phase(nc, keep)
                attention_phase(nc, keep, 1)
            parked = nc.dram_tensor("parked_x", [P, ALL_TILES, P], F32).ap()
            parked_done = mx.sem("parked_done")
            with nc.Block() as block:

                @block.sync
                def _(sp):
                    sp.dma_start(parked, keep.xres[:]).then_inc(parked_done, 16)
                    sp.wait_ge(parked_done, 16)
        local_phase(nc, keep)
        output_phase(nc, keep, parked, out)


LOCAL_ORDER = ["QK0", 0, "QK1", 1, "T0", 2, "QK2", "PV0", 3, "T1", "QK3", 4, "PV1", "T2", 5, "TZ0", "PV2", 6,
               "T3", 7, "PV3", 8, "TZ1", 9, "WO", 10]
FRONT = list(range(11))
T_INDEX = {"T0": 0, "T1": 1, "T2": 2, "TZ0": 3, "T3": 4, "TZ1": 5}
Z_INDEX = {"PV0": 0, "PV1": 1, "PV2": 2, "PV3": 3, "WO": 4}
FF_LAG = 3
HALF = DIM // 2


def local_phase(nc, keep):
    UC = [(0, P), (P, P), (2 * P, DIM_INNER - 2 * P)]
    with ExitStack() as ctx:
        m = Mem(nc, ctx)
        wqkv = m.sb("lo_wqkv", [P, 2, 3 * INNER])
        wo = m.sb("lo_wo", [P, 2, INNER])
        w1 = m.sb("lo_w1", [P, 2, 2 * DIM_INNER])
        w2 = m.sb("lo_w2", [P, 2, 3 * P])
        b1 = m.sb("lo_b1", [P, 2, 2 * DIM_INNER])
        b2 = m.sb("lo_b2", [P, 2, DIM])
        ln = m.sb("lo_ln", [P, DEPTH, 2])
        scales = m.sb("lo_scales", [P, DEPTH + 1, 4, LOC_HD])
        rotary = m.sb("lo_rotary", [P, 4, TILES, LOC_HD])
        tables = m.sb("lo_tables", [P, 4, TILES, LOC_HD])
        mask = m.sb("lo_mask", [P, TILES, LOC_KEYS], BF16)
        has_prev = m.sb("lo_has_prev", [P, TILES])
        shift = m.sb("lo_shift", [P, 2, P])
        rows = [m.sb(f"lo_rows{s}", [P, P]) for s in range(2)]
        prev = [m.sb(f"lo_prev{s}", [P, HALF]) for s in range(2)]
        xT = [m.sb(f"lo_xT{s}", [P, P]) for s in range(2)]
        qT = [m.sb(f"lo_qT{s}", [P, PAIRS, P]) for s in range(2)]
        kT = [m.sb(f"lo_kT{s}", [P, PAIRS, LOC_KEYS]) for s in range(2)]
        val = [m.sb(f"lo_val{s}", [P, HEADS, VW]) for s in range(2)]
        tail = [m.sb(f"lo_tail{s}", [P, GROUPS, GROUP, VW]) for s in range(2)]
        square = m.sb("lo_square", [P, 2, 512])
        by_cos = m.sb("lo_by_cos", [P, 2, 512])
        by_sin = m.sb("lo_by_sin", [P, 2, 512])
        rot = m.sb("lo_rot", [P, 4, 8, LOC_HD])
        unit = m.sb("lo_unit", [P, 4, 8, LOC_HD])
        sumsq = m.sb("lo_sumsq", [P, 4, 8])
        norm = m.sb("lo_norm", [P, 4, 8])
        rnorm = m.sb("lo_rnorm", [P, 4, 8])
        row_max = m.sb("lo_row_max", [P, 2, GROUP])
        diff = m.sb("lo_diff", [P, 2, GROUP, LOC_KEYS])
        prob = m.sb("lo_prob", [P, 2, GROUP, P])
        prob_prev = m.sb("lo_prob_prev", [WINDOW, 2, GROUP, WINDOW])
        probT = m.sb("lo_probT", [P, 2, GROUP, P])
        tailT = m.sb("lo_tailT", [P, 2, WINDOW])
        rden = m.sb("lo_rden", [P, GROUP])
        zn = m.sb("lo_zn", [P, HEADS, LOC_HD])
        znT = m.sb("lo_znT", [P, PAIRS, P])
        xs = m.sb("ff_xs", [P, 2, P])
        stats = m.sb("ff_stats", [P, 6])
        meanvar = m.sb("ff_meanvar", [P, 2, 2])
        var = m.sb("ff_var", [P, 1])
        rstd = m.sb("ff_rstd", [P, 1])
        xn = m.sb("ff_xn", [P, 2, P])
        xnT = m.sb("ff_xnT", [P, 2, P])
        a_sb, gate, gelu = (b[:, :, 0:DIM_INNER] for b in (square, by_cos, by_sin))
        prod = rot[:].rearrange("p (s c) h d -> p s (c h d)", s=2)[:, :, 0:DIM_INNER]
        prodT = probT[:, :, 0:3, :]
        yb = m.sb("ff_yb", [P, 2, P])
        ps = m.ps("lo_ps", [P, 8, 512])
        S_BANK, T_BANK, Z_BANK, F_BANK = 0, 4, 5, 6
        A_BANK, B_BANK, H_BANK, D_BANK, E_BANK = 0, 1, 2, 6, 7

        sem = {}

        def S(name):
            if name not in sem:
                sem[name] = m.sem("lo_" + name)
            return sem[name]

        loaded, consts, tables_done = S("loaded"), S("consts"), S("tables_done")
        w_loaded = S("w_loaded")
        rows_staged, xT_done = S("rows_staged"), S("xT_done")
        f_filled, f_free = [S(f"f_filled{k}") for k in range(2)], [S(f"f_free{k}") for k in range(2)]
        squared, rot_parts, sumsq_done, rot_done = S("squared"), S("rot_parts"), S("sumsq_done"), S("rot_done")
        clamped, rnorm_done, unit_done = S("clamped"), S("rnorm_done"), S("unit_done")
        tail_done = [S(f"tail_done{k}") for k in range(2)]
        val_done, qkT_done, kprev_done = S("val_done"), S("qkT_done"), S("kprev_done")
        prev_exp_done = S("prev_exp_done")
        scored, max_done, diff_done, exp_done = S("scored"), S("max_done"), S("diff_done"), S("exp_done")
        t_filled, t_free, tailT_done = S("t_filled"), S("t_free"), S("tailT_done")
        z_filled, z_free, rden_done, zn_done, znT_done = S("z_filled"), S("z_free"), S("rden_done"), S("zn_done"), S("znT_done")
        mid_done, out_done = S("mid_done"), S("out_done")
        a_filled, xs_half, xs_done, stats_done, mv_done = S("a_filled"), S("xs_half"), S("xs_done"), S("stats_done"), S("mv_done")
        var_done, rstd_done, xn_done, b_filled, xnT_done = S("var_done"), S("rstd_done"), S("xn_done"), S("b_filled"), S("xnT_done")
        h_filled, a_done, gate_done, gelu_done, prod_done = S("h_filled"), S("a_done"), S("gate_done"), S("gelu_done"), S("prod_done")
        d_filled, prodT_done, e_filled, yb_done = S("d_filled"), S("prodT_done"), S("e_filled"), S("yb_done")
        W_DMAS = 7

        def slot_of(tile):
            return tile + (tile >> 3) + 1

        def at(buf, tile, back=0):
            return buf[:, bass.ds(slot_of(tile) - back, 1), :].rearrange("p a c -> p (a c)")

        def attention_steps(eng, l, front, back):
            def steps(tile_b, tile_f, par):
                for piece in LOCAL_ORDER:
                    if isinstance(piece, int):
                        if tile_f is not None:
                            front(l, tile_f, 1 - par, piece)
                    else:
                        back(l, tile_b, par, piece)
            for k in FRONT:
                front(l, 0, 0, k)
            with eng.Fori(0, ALL_TILES // 2 - 1) as i:
                steps(2 * i, 2 * i + 1, 0)
                steps(2 * i + 1, 2 * i + 2, 1)
            steps(ALL_TILES - 2, ALL_TILES - 1, 0)
            steps(ALL_TILES - 1, None, 1)

        def ff_steps(eng, l, step):
            def one(s, par):
                known = isinstance(s, int)
                step(l,
                     s if not known or s < ALL_TILES else None,
                     s - 1 if not known or 0 <= s - 1 < ALL_TILES else None,
                     s - FF_LAG if not known or s - FF_LAG >= 0 else None, par)
            for s in range(4):
                one(s, s % 2)
            with eng.Fori(2, ALL_TILES // 2) as i:
                one(2 * i, 0)
                one(2 * i + 1, 1)
            for s in range(ALL_TILES, ALL_TILES + FF_LAG):
                one(s, s % 2)

        with nc.Block() as block:

            @block.sync
            def _(sp):
                for dst, src in ((ln, "ln"), (rotary, "lo_rotary"), (mask, "lo_mask"), (shift, "lo_shift")):
                    sp.dma_start(dst[:], keep.dram[src]).then_inc(loaded, 16)
                sp.dma_start(scales[:, 0:DEPTH], keep.dram["lo_scales"].rearrange("(a l) k d -> a l k d", a=1).broadcast_to([P, DEPTH, 4, LOC_HD])).then_inc(loaded, 16)

                def load_layer(l, slot):
                    one = bass.ds(l, 1)
                    for dst, name in ((wqkv, "Wqkv"), (w1, "W1")):
                        sp.dma_start(dst[:, slot, :], keep.dram[name][one].rearrange("a p n -> p (a n)")).then_inc(w_loaded, 16)
                    sp.dma_start(wo[:, slot, :].rearrange("p (k e) -> p k e", e=DIM),
                                 keep.dram["Wo"][one].rearrange("a (k p) e -> p (a k) e", p=P)).then_inc(w_loaded, 16)
                    sp.dma_start(w2[:, slot, 0:2 * P].rearrange("p (k e) -> p k e", e=DIM),
                                 keep.dram["W2"][one, 0:2 * P].rearrange("a (k p) e -> p (a k) e", p=P)).then_inc(w_loaded, 16)
                    sp.dma_start(w2[0:UC[2][1], slot, 2 * P:], keep.dram["W2"][one, 2 * P:].rearrange("a p e -> p (a e)")).then_inc(w_loaded, 16)
                    sp.dma_start(b1[:, slot, :], keep.dram["b1"][one].broadcast_to([P, 2 * DIM_INNER])).then_inc(w_loaded, 16)
                    sp.dma_start(b2[:, slot, :], keep.dram["b2"][one].broadcast_to([P, DIM])).then_inc(w_loaded, 16)

                def tails(l, tile, par):
                    n = l * ALL_TILES + tile
                    sp.wait_ge(val_done, 2 * n + 2)
                    sp.wait_ge(zn_done, 4 * n + 4)
                    v = val[1 - par][P - WINDOW:P].rearrange("p (g j) d -> p g j d", j=GROUP)
                    for j in range(GROUP):
                        sp.dma_start(tail[par][j * WINDOW:(j + 1) * WINDOW, :, j, :], v[:, :, j, :]).then_inc(tail_done[par], 16)

                load_layer(0, 0)
                sp.wait_ge(consts, 1)

                def layer(l, par, more):
                    with sp.Fori(0, ALL_TILES // 2) as i:
                        tails(l, 2 * i, 0)
                        tails(l, 2 * i + 1, 1)
                    if more:
                        sp.wait_ge(mid_done, l * ALL_TILES + 1)
                        load_layer(l + 1, 1 - par)
                    sp.wait_ge(out_done, (l + 1) * ALL_TILES + 2)
                    sp.nop(nofuse=True)
                with sp.Fori(0, DEPTH // 2 - 1) as h:
                    layer(2 * h, 0, True)
                    layer(2 * h + 1, 1, True)
                layer(DEPTH - 2, 0, True)
                layer(DEPTH - 1, 1, False)
                for k in range(2):
                    sp.wait_ge(tail_done[k], 16 * GROUP * DEPTH * ALL_TILES // 2)
                sp.wait_ge(w_loaded, 16 * W_DMAS * DEPTH)

            @block.gpsimd
            def _(pool):
                for s in range(2):
                    pool.memset(tail[s][:], 0.0).then_inc(S("pool_init"), 1)
                    pool.memset(val[s][:], 1.0).then_inc(S("pool_init"), 1)
                    pool.memset(kT[s][:], 0.0).then_inc(S("pool_init"), 1)
                pool.memset(scales[:, DEPTH], 0.0).then_inc(S("pool_init"), 1)
                pool.memset(has_prev[:, 0:1], 0.0).then_inc(S("pool_init"), 1)
                pool.memset(has_prev[:, 1:TILES], 1.0).then_inc(S("pool_init"), 1)
                pool.wait_ge(S("pool_init"), 9)
                pool.sem_inc(consts, 1)
                pool.sem_inc(unit_done, 1)
                pool.wait_ge(loaded, 80)

                def make_tables(l):
                    for k in range(4):
                        pool.tensor_tensor(tables[:, k], rotary[:, k],
                                           scales[:, bass.ds(l, 1), k].rearrange("p a d -> p a d").broadcast_to([P, TILES, LOC_HD]),
                                           ALU.mult).then_inc(tables_done, 1)

                def front(l, tile, par, k):
                    n = l * ALL_TILES + tile
                    if k == 0:
                        pool.wait_ge(xT_done, n + 1)
                        pool.nop(nofuse=True)
                        pool.tensor_copy(rows[par][:], at(keep.y_in, tile)).then_inc(rows_staged, 1)
                        pool.tensor_copy(prev[par][:], at(keep.y_in, tile, 1)[:, HALF:]).then_inc(rows_staged, 1)
                    if 1 <= k <= 4:
                        pool.wait_ge(rot_parts, 3 * (4 * n + k))
                        pool.tensor_tensor(rot[:, k - 1].rearrange("p h d -> p (h d)"), by_cos[:, k % 2], by_sin[:, k % 2], ALU.add).then_inc(rot_done, 1)
                    if k in (2, 4):
                        a, b = k - 2, k
                        pool.wait_ge(sumsq_done, 4 * n + k)
                        pool.nop(nofuse=True)
                        pool.tensor_scalar(norm[:, a:b], sumsq[:, a:b], 1e-24, None, ALU.max).then_inc(clamped, 1)
                        pool.wait_ge(clamped, 2 * n + k // 2)
                        pool.tensor_tensor(rnorm[:, a:b].rearrange("p c h -> p (c h)"), norm[:, a:b].rearrange("p c h -> p (c h)"),
                                           keep.neg_half[:, 0:2 * 8], ALU.pow).then_inc(rnorm_done, 1)
                        pool.wait_ge(rnorm_done, 2 * n + k // 2)
                        pool.wait_ge(rot_done, 4 * n + k + 2)
                        pool.wait_ge(f_free[0], 6 * n + 1)
                        pool.wait_ge(f_free[1], 5 * n + 1)
                        pool.tensor_tensor(unit[:, a:b].rearrange("p c h d -> p (c h) d"), rot[:, a:b].rearrange("p c h d -> p (c h) d"),
                                           rnorm[:, a:b].rearrange("p c (h x) -> p (c h) x", x=1).broadcast_to([P, 16, LOC_HD]),
                                           ALU.mult).then_inc(unit_done, 1)
                    if k == 8:
                        pool.wait_ge(qkT_done, 4 * n + 4)
                        pool.wait_ge(diff_done, 4 * n + 4)
                        pool.nop(nofuse=True)
                        pool.tensor_tensor(kT[par][:, :, 0:WINDOW], kT[1 - par][:, :, P:LOC_KEYS],
                                           has_prev[:, bass.ds(tile & (TILES - 1), 1)].rearrange("p (a b) -> p a b", b=1).broadcast_to([P, PAIRS, WINDOW]),
                                           ALU.mult).then_inc(kprev_done, 1)

                def ff(l, sa, sc, sd, par):
                    if sa is not None:
                        n = l * ALL_TILES + sa
                        pool.wait_ge(xn_done, n + 1)
                        pool.nop(nofuse=True)
                        pool.tensor_copy(xs[:, par, 0:HALF], at(keep.y_mid, sa)[:, 0:HALF]).then_inc(xs_half, 1)
                        pool.wait_ge(mv_done, n + 1)
                        pool.nop(nofuse=True)
                        pool.tensor_scalar(var[:], meanvar[:, par, 1:2], LN_EPS, None, ALU.add).then_inc(var_done, 1)
                        pool.wait_ge(var_done, n + 1)
                        pool.tensor_tensor(rstd[:], var[:], keep.neg_half[:, 0:1], ALU.pow).then_inc(rstd_done, 1)
                    if sc is not None:
                        n = l * ALL_TILES + sc
                        q = 1 - par
                        pool.wait_ge(a_done, n + 3)
                        pool.wait_ge(gelu_done, n + 1)
                        pool.wait_ge(prodT_done, n + 1)
                        pool.tensor_tensor(prod[:, q], a_sb[:, q], gelu[:, q], ALU.mult).then_inc(prod_done, 1)
                    if sd is not None:
                        n = l * ALL_TILES + sd
                        q = 1 - par
                        pool.wait_ge(out_done, n + 1)
                        pool.nop(nofuse=True)
                        pool.tensor_tensor(yb[:, q], at(keep.y_mid, sd), b2[:, bass.ds(l & 1, 1)].rearrange("p a c -> p (a c)"), ALU.add).then_inc(yb_done, 1)

                pool.sem_inc(prodT_done, 2)
                pool.sem_inc(xn_done, 2)
                pool.sem_inc(yb_done, 1)
                pool.sem_inc(prod_done, 2)
                pool.sem_inc(rot_done, 2)
                make_tables(0)
                with pool.Fori(0, DEPTH) as l:
                    pool.wait_ge(w_loaded, (l + 1) * 16 * W_DMAS)
                    attention_steps(pool, l, front, lambda *_: None)
                    pool.wait_ge(mid_done, (l + 1) * ALL_TILES)
                    make_tables(l + 1)
                    ff_steps(pool, l, ff)
                    pool.wait_ge(out_done, (l + 1) * ALL_TILES + 2)

            @block.tensor
            def _(pe):
                def front(l, tile, par, k):
                    n = l * ALL_TILES + tile
                    bank = ps[:, F_BANK + k % 2, :]
                    pe.wait_ge(f_free[k % 2], n * (6 - k % 2) + k // 2 + 1)
                    if k == 0:
                        pe.wait_ge(rows_staged, 2 * n + 2)
                        pe.matmul(bank[0:HALF, 0:P], rows[par][:, 0:HALF], keep.ident[:], start=True, stop=True)
                        pe.matmul(bank[HALF:P, 0:P], rows[par][:, HALF:], shift[:, 0, :], start=True, stop=False)
                        last = pe.matmul(bank[HALF:P, 0:P], prev[par][:], shift[:, 1, :], start=False, stop=True)
                    elif k <= 6:
                        if k == 1:
                            pe.wait_ge(xT_done, n + 3)
                        last = pe.matmul(bank[:], xT[par][:], wqkv[:, bass.ds(l & 1, 1), (k - 1) * 512:k * 512].rearrange("p a n -> p (a n)"),
                                         start=True, stop=True)
                    else:
                        pe.wait_ge(unit_done, 2 * n + (k - 7) // 2 + 2)
                        c = unit[:, k - 7].rearrange("p h d -> p (h d)")
                        for j in range(4):
                            last = pe.transpose(bank[:, j * P:(j + 1) * P], c[:, j * P:(j + 1) * P], keep.ident[:])
                    last.then_inc(f_filled[k % 2], 1)

                def back(l, tile, par, piece):
                    n = l * ALL_TILES + tile
                    kind, g = piece.rstrip("0123"), int(piece[-1]) if piece[-1].isdigit() else 0
                    u = 4 * n + g
                    sl = g % 2
                    scores = ps[:, S_BANK + 2 * sl:S_BANK + 2 * sl + 2, :]
                    if kind == "QK":
                        if g == 0:
                            pe.wait_ge(qkT_done, 4 * n + 8)
                            pe.wait_ge(kprev_done, n + 1)
                        pe.wait_ge(tailT_done, u + 1)
                        for j in range(GROUP):
                            h = 4 * g + j
                            r = slice(64 * (h % 2), 64 * (h % 2) + 64)
                            o = scores[:, j % 2, (j // 2) * LOC_KEYS:(j // 2 + 1) * LOC_KEYS]
                            pe.matmul(o, qT[par][r, h // 2, :], kT[par][r, h // 2, :], start=True, stop=False)
                            last = pe.matmul(o, keep.identb[:], mask[:, bass.ds(tile & (TILES - 1), 1), :].rearrange("p a k -> p (a k)"),
                                             start=False, stop=True)
                        last.then_inc(scored, 1)
                    elif kind == "T":
                        pe.wait_ge(exp_done, u + 3)
                        pe.wait_ge(t_free, 6 * n + T_INDEX[piece] + 1)
                        for j in range(GROUP):
                            pe.transpose(ps[:, T_BANK, j * P:(j + 1) * P], prob[:, sl, j, :], keep.ident[:])
                        last = pe.transpose(scores[:, 0, 2 * LOC_KEYS:2 * LOC_KEYS + WINDOW], prob_prev[:, sl].rearrange("p j k -> p (j k)"), keep.ident[0:WINDOW, 0:WINDOW])
                        last.then_inc(t_filled, 1)
                    elif kind == "PV":
                        pe.wait_ge(t_free, 6 * n + T_INDEX[f"T{g}"] + 2)
                        pe.wait_ge(tailT_done, u + 3)
                        pe.wait_ge(z_free, 5 * n + g + 1)
                        if g == 0:
                            pe.wait_ge(val_done, 2 * n + 4)
                            pe.wait_ge(tail_done[par], 16 * GROUP * (n >> 1) + 16 * GROUP)
                        for j in range(GROUP):
                            pe.matmul(ps[:, Z_BANK, j * VW:(j + 1) * VW], probT[:, sl, j, :], val[par][:, 4 * g + j, :],
                                      start=(j == 0), stop=False, skip_group_check=True)
                        last = pe.matmul(ps[0:WINDOW, Z_BANK, 0:GROUP * VW], tailT[:, sl, :], tail[par][:, g].rearrange("p j d -> p (j d)"),
                                         start=False, stop=True, skip_group_check=True)
                        last.then_inc(z_filled, 1)
                    elif kind == "TZ":
                        pe.wait_ge(zn_done, 4 * n + 8 + 2 * g + 2)
                        pe.wait_ge(t_free, 6 * n + T_INDEX[piece] + 1)
                        flat = zn[:].rearrange("p h d -> p (h d)")
                        for j in range(4):
                            last = pe.transpose(ps[:, T_BANK, j * P:(j + 1) * P], flat[:, (4 * g + j) * P:(4 * g + j + 1) * P], keep.ident[:])
                        last.then_inc(t_filled, 1)
                    else:
                        pe.wait_ge(znT_done, 2 * n + 2)
                        pe.wait_ge(z_free, 5 * n + Z_INDEX["WO"] + 1)
                        for c in range(PAIRS):
                            last = pe.matmul(ps[:, Z_BANK, 0:P], znT[:, c, :], wo[:, bass.ds(l & 1, 1), c * P:(c + 1) * P].rearrange("p a n -> p (a n)"),
                                             start=(c == 0), stop=(c == PAIRS - 1))
                        last.then_inc(z_filled, 1)

                def ff(l, sa, sc, sd, par):
                    q = 1 - par
                    if sa is not None:
                        n = l * ALL_TILES + sa
                        pe.wait_ge(xs_done, n + 1)
                        pe.matmul(ps[:, A_BANK, 0:HALF], shift[:, 0, :], at(keep.y_mid, sa)[:, HALF:], start=True, stop=False)
                        pe.matmul(ps[:, A_BANK, 0:HALF], shift[:, 1, :], at(keep.y_mid, sa, 1)[:, HALF:], start=False, stop=True).then_inc(a_filled, 1)
                    if sd is not None:
                        n = l * ALL_TILES + sd
                        pe.wait_ge(prod_done, n + 3)
                        for c, (o, w) in enumerate(UC):
                            last = pe.transpose(ps[0:w, D_BANK, c * P:(c + 1) * P], prod[:, q, o:o + w], keep.ident[:])
                        last.then_inc(d_filled, 1)
                    if sc is not None:
                        n = l * ALL_TILES + sc
                        pe.wait_ge(xn_done, n + 3)
                        pe.transpose(ps[:, B_BANK, 0:P], xn[:, q], keep.ident[:]).then_inc(b_filled, 1)
                        pe.wait_ge(xnT_done, n + 1)
                        pe.wait_ge(a_done, n + 1)
                        for k in range(2):
                            last = pe.matmul(ps[:, H_BANK + 2 * q + k, 0:DIM_INNER], xnT[:, q],
                                             w1[:, bass.ds(l & 1, 1), k * DIM_INNER:(k + 1) * DIM_INNER].rearrange("p a n -> p (a n)"), start=True, stop=True)
                        last.then_inc(h_filled, 1)
                    if sd is not None:
                        n = l * ALL_TILES + sd
                        pe.wait_ge(prodT_done, n + 3)
                        pe.wait_ge(out_done, n + 2)
                        for c, (o, w) in enumerate(UC):
                            last = pe.matmul(ps[:, E_BANK, 0:P], prodT[0:w, q, c, :], w2[0:w, bass.ds(l & 1, 1), c * P:(c + 1) * P].rearrange("p a n -> p (a n)"),
                                             start=(c == 0), stop=(c == 2))
                        last.then_inc(e_filled, 1)

                pe.wait_ge(loaded, 80)
                with pe.Fori(0, DEPTH) as l:
                    pe.wait_ge(w_loaded, (l + 1) * 16 * W_DMAS)
                    attention_steps(pe, l, front, back)
                    pe.wait_ge(mid_done, (l + 1) * ALL_TILES)
                    ff_steps(pe, l, ff)
                    pe.wait_ge(out_done, (l + 1) * ALL_TILES + 2)

            @block.vector
            def _(dve):
                dve.wait_ge(loaded, 80)
                dve.sem_inc(f_free[0], 1)
                dve.sem_inc(f_free[1], 1)
                dve.sem_inc(diff_done, 8)
                dve.sem_inc(z_free, 1)
                dve.sem_inc(zn_done, 8)
                dve.sem_inc(xs_done, 1)
                dve.sem_inc(a_done, 2)
                dve.sem_inc(out_done, 2)
                dve.wait_ge(tables_done, 4)

                def front(l, tile, par, k):
                    if not 1 <= k <= 4:
                        return
                    n = l * ALL_TILES + tile
                    c = 4 * n + k - 1
                    t = tile & (TILES - 1)
                    rows_q = ps[:, F_BANK + k % 2, :].rearrange("p (h d) -> p h d", d=LOC_HD)
                    side = 2 * ((k - 1) // 2)
                    h = LOC_HD // 2

                    def table(which, lo, hi):
                        tab = tables[:].rearrange("p k t d -> p (k t) d")[:, bass.ds((side + which) * TILES + t, 1), lo:hi]
                        return tab.broadcast_to([P, 8, hi - lo])

                    if k == 1:
                        dve.wait_ge(tables_done, 4 * l + 4)
                    dve.wait_ge(squared, c + 1)
                    dve.wait_ge(rot_done, c + 1)
                    oc = by_cos[:, k % 2].rearrange("p (h d) -> p h d", d=LOC_HD)
                    os_ = by_sin[:, k % 2].rearrange("p (h d) -> p h d", d=LOC_HD)
                    dve.tensor_tensor(oc, rows_q, table(0, 0, LOC_HD), ALU.mult).then_inc(rot_parts, 1)
                    dve.tensor_tensor(os_[:, :, 0:h], rows_q[:, :, h:], table(1, 0, h), ALU.mult).then_inc(rot_parts, 1)
                    dve.tensor_tensor(os_[:, :, h:], rows_q[:, :, 0:h], table(1, h, LOC_HD), ALU.mult).then_inc(rot_parts, 1)
                    dve.tensor_reduce(sumsq[:, k - 1, :], square[:, k % 2].rearrange("p (h d) -> p h d", d=LOC_HD), AX.X, ALU.add).then_inc(sumsq_done, 1)
                    dve.wait_ge(rot_parts, 3 * (c + 1))
                    dve.sem_inc(f_free[k % 2], 1)

                def back(l, tile, par, piece):
                    n = l * ALL_TILES + tile
                    kind, g = piece.rstrip("0123"), int(piece[-1]) if piece[-1].isdigit() else 0
                    u = 4 * n + g
                    sl = g % 2
                    if kind == "QK":
                        s4 = ps[:, S_BANK + 2 * sl:S_BANK + 2 * sl + 2, 0:2 * LOC_KEYS].rearrange("p b (j k) -> p b j k", k=LOC_KEYS)
                        dve.wait_ge(scored, u + 1)
                        dve.tensor_reduce(row_max[:, sl, :].rearrange("p (b j) -> p b j", b=2), s4, AX.X, ALU.max).then_inc(max_done, 1)
                        dve.wait_ge(max_done, u + 1)
                        dve.wait_ge(exp_done, u + 1)
                        dve.tensor_tensor(diff[:, sl].rearrange("p (j b) k -> p b j k", b=2), s4,
                                          row_max[:, sl, :].rearrange("p (b j x) -> p b j x", b=2, x=1).broadcast_to([P, 2, 2, LOC_KEYS]),
                                          ALU.subtract).then_inc(diff_done, 1)
                    elif kind == "PV":
                        z = ps[:, Z_BANK, 0:GROUP * VW].rearrange("p (j d) -> p j d", d=VW)
                        dve.wait_ge(z_filled, 5 * n + g + 1)
                        dve.reciprocal(rden[:].rearrange("p (j x) -> p j x", x=1), z[:, :, LOC_HD:VW]).then_inc(rden_done, 1)
                        dve.wait_ge(rden_done, u + 1)
                        dve.tensor_tensor(zn[:, 4 * g:4 * g + 4, :], z[:, :, 0:LOC_HD],
                                          rden[:].rearrange("p (j x) -> p j x", x=1).broadcast_to([P, GROUP, LOC_HD]), ALU.mult).then_inc(zn_done, 1)
                        dve.wait_ge(zn_done, u + 9)
                        dve.sem_inc(z_free, 1)
                    elif kind == "WO":
                        dve.wait_ge(z_filled, 5 * n + 5)
                        dve.tensor_tensor(at(keep.y_mid, tile), ps[:, Z_BANK, 0:P], at(keep.y_in, tile), ALU.add).then_inc(mid_done, 1)
                        dve.wait_ge(mid_done, n + 1)
                        dve.sem_inc(z_free, 1)

                def ff(l, sa, sc, sd, par):
                    q = 1 - par
                    if sa is not None:
                        n = l * ALL_TILES + sa
                        dve.wait_ge(a_filled, n + 1)
                        dve.wait_ge(xn_done, n + 1)
                        dve.tensor_copy(xs[:, par, HALF:], ps[:, A_BANK, 0:HALF]).then_inc(xs_done, 1)
                        dve.wait_ge(xs_done, n + 2)
                        dve.wait_ge(xs_half, n + 1)
                        dve.bn_stats(stats[:], xs[:, par]).then_inc(stats_done, 1)
                        dve.wait_ge(stats_done, n + 1)
                        dve.nop(nofuse=True)
                        dve.bn_aggr(meanvar[:, par], stats[:]).then_inc(mv_done, 1)
                    if sc is not None:
                        n = l * ALL_TILES + sc
                        dve.wait_ge(h_filled, n + 1)
                        bias = b1[:, bass.ds(l & 1, 1)].rearrange("p a n -> p (a n)")
                        dve.wait_ge(prod_done, n + 1)
                        dve.tensor_tensor(gate[:, q], ps[:, H_BANK + 2 * q + 1, 0:DIM_INNER], bias[:, DIM_INNER:], ALU.add).then_inc(gate_done, 1)
                        dve.tensor_tensor(a_sb[:, q], ps[:, H_BANK + 2 * q, 0:DIM_INNER], bias[:, 0:DIM_INNER], ALU.add).then_inc(a_done, 1)
                    if sa is not None:
                        n = l * ALL_TILES + sa
                        dve.wait_ge(rstd_done, n + 1)
                        dve.tensor_scalar(xn[:, par], xs[:, par], meanvar[:, par, 0:1], rstd[:], ALU.subtract, ALU.mult).then_inc(xn_done, 1)
                    if sd is not None:
                        n = l * ALL_TILES + sd
                        dve.wait_ge(e_filled, n + 1)
                        dve.wait_ge(yb_done, n + 2)
                        dve.tensor_tensor(at(keep.y_in, sd), ps[:, E_BANK, 0:P], yb[:, q], ALU.add).then_inc(out_done, 1)

                with dve.Fori(0, DEPTH) as l:
                    dve.wait_ge(w_loaded, (l + 1) * 16 * W_DMAS)
                    attention_steps(dve, l, front, back)
                    dve.wait_ge(mid_done, (l + 1) * ALL_TILES)
                    ff_steps(dve, l, ff)
                    dve.wait_ge(out_done, (l + 1) * ALL_TILES + 2)

            @block.scalar
            def _(act):
                act.wait_ge(consts, 1)
                act.sem_inc(xT_done, 2)
                act.sem_inc(val_done, 2)
                act.sem_inc(qkT_done, 4)
                act.sem_inc(exp_done, 2)
                act.sem_inc(t_free, 1)
                act.sem_inc(tailT_done, 2)

                def front(l, tile, par, k):
                    n = l * ALL_TILES + tile
                    bank = ps[:, F_BANK + k % 2, :]
                    act.wait_ge(f_filled[k % 2], n * (6 - k % 2) + k // 2 + 1)
                    if k == 0:
                        act.copy(xT[par][:], bank[:, 0:P]).then_inc(xT_done, 1)
                        act.wait_ge(xT_done, n + 3)
                    elif k <= 4:
                        c = 4 * n + k - 1
                        act.wait_ge(sumsq_done, c) if k > 1 else None
                        act.activation(square[:, k % 2], bank[:], ACT.Square).then_inc(squared, 1)
                        return
                    elif k <= 6:
                        act.copy(val[par][:, 8 * (k - 5):8 * (k - 4), 0:LOC_HD], bank[:].rearrange("p (h d) -> p h d", d=LOC_HD)).then_inc(val_done, 1)
                        act.wait_ge(val_done, 2 * n + k - 5 + 3)
                    else:
                        j = k - 7
                        src = bank[:].rearrange("p (h t) -> p h t", t=P)
                        dst = qT[par][:, 4 * j:4 * j + 4, :] if j < 2 else kT[par][:, 4 * (j - 2):4 * (j - 2) + 4, WINDOW:]
                        act.copy(dst, src).then_inc(qkT_done, 1)
                        act.wait_ge(qkT_done, 4 * n + j + 5)
                    act.sem_inc(f_free[k % 2], 1)

                def back(l, tile, par, piece):
                    n = l * ALL_TILES + tile
                    kind, g = piece.rstrip("0123"), int(piece[-1]) if piece[-1].isdigit() else 0
                    u = 4 * n + g
                    sl = g % 2
                    if kind == "T":
                        act.wait_ge(diff_done, u + 9)
                        act.activation(prob_prev[:, sl], diff[0:WINDOW, sl, :, 0:WINDOW], ACT.Exp, scale=QK_SCALE).then_inc(prev_exp_done, 1)
                        act.activation(prob[:, sl], diff[:, sl, :, WINDOW:], ACT.Exp, scale=QK_SCALE).then_inc(exp_done, 1)
                        act.wait_ge(t_filled, 6 * n + T_INDEX[piece] + 1)
                        act.wait_ge(zn_done, u + 7)
                        act.copy(tailT[:, sl], ps[:, S_BANK + 2 * sl, 2 * LOC_KEYS:2 * LOC_KEYS + WINDOW]).then_inc(tailT_done, 1)
                        act.copy(probT[:, sl], ps[:, T_BANK, :].rearrange("p (j q) -> p j q", q=P)).then_inc(t_free, 1)
                    elif kind == "TZ":
                        act.wait_ge(t_filled, 6 * n + T_INDEX[piece] + 1)
                        act.wait_ge(z_free, 5 * n + 1)
                        act.copy(znT[:, 4 * g:4 * g + 4, :], ps[:, T_BANK, :].rearrange("p (j q) -> p j q", q=P)).then_inc(znT_done, 1)
                        act.wait_ge(znT_done, 2 * n + g + 1)
                        act.sem_inc(t_free, 1)

                def ff(l, sa, sc, sd, par):
                    q = 1 - par
                    if sd is not None:
                        n = l * ALL_TILES + sd
                        act.wait_ge(d_filled, n + 1)
                        act.copy(prodT[:, q, 0:2], ps[:, D_BANK, 0:2 * P].rearrange("p (c t) -> p c t", t=P))
                        act.copy(prodT[0:UC[2][1], q, 2], ps[0:UC[2][1], D_BANK, 2 * P:3 * P]).then_inc(prodT_done, 1)
                    if sc is not None:
                        n = l * ALL_TILES + sc
                        act.wait_ge(b_filled, n + 1)
                        act.nop(nofuse=True)
                        act.activation(xnT[:, q], ps[:, B_BANK, 0:P], ACT.Identity, bias=ln[:, bass.ds(l, 1), 1:2].rearrange("p a b -> p (a b)"),
                                       scale=ln[:, bass.ds(l, 1), 0:1].rearrange("p a b -> p (a b)")).then_inc(xnT_done, 1)
                        act.wait_ge(gate_done, n + 1)
                        act.activation(gelu[:, q], gate[:, q], ACT.Gelu).then_inc(gelu_done, 1)

                with act.Fori(0, DEPTH) as l:
                    attention_steps(act, l, front, back)
                    act.wait_ge(mid_done, (l + 1) * ALL_TILES)
                    ff_steps(act, l, ff)
                    act.wait_ge(out_done, (l + 1) * ALL_TILES + 2)


def output_phase(nc, keep, parked, out):
    with ExitStack() as ctx:
        m = Mem(nc, ctx)
        x = m.sb("out_x", [P, ALL_TILES, P])
        summed, stored = m.sem("summed"), m.sem("stored")
        fetched = [m.sem(f"fetched{b}") for b in range(BATCH)]
        with nc.Block() as block:

            @block.vector
            def _(dve):
                for b in range(BATCH):
                    row = x[:, b * TILES:(b + 1) * TILES, :]
                    first = b * (TILES + 1) + 1
                    dve.wait_ge(fetched[b], 16)
                    dve.tensor_tensor(row, row, keep.y_in[:, first:first + TILES, :], ALU.add).then_inc(summed, 1)

            @block.sync
            def _(sp):
                for b in range(BATCH):
                    part = slice(b * TILES, (b + 1) * TILES)
                    sp.dma_start(x[:, part, :], parked[:, part, :]).then_inc(fetched[b], 16)
                for b in range(BATCH):
                    sp.wait_ge(summed, b + 1)
                    sp.dma_start(out.rearrange("b (t p) c -> p b t c", p=P)[:, b], x[:, b * TILES:(b + 1) * TILES, :]).then_inc(stored, 16)
                sp.wait_ge(stored, 16 * BATCH)


def rotary_angles(n, hd, np):
    half = np.arange(0, hd, 2, dtype=np.float32)
    inv = (1.0 / np.power(np.float32(10000.0), half / np.float32(hd))).astype(np.float32)
    f = np.arange(n, dtype=np.float32)[:, None] * inv[None, :]
    return np.concatenate([f, f], -1), half


def shape_tables(np):
    t = {}
    by_tile = lambda a: np.ascontiguousarray(a.reshape(TILES, P, -1).transpose(1, 0, 2))
    f, _ = rotary_angles(SEQ, L1_HD, np)
    sign = np.where(np.arange(L1_HD) < L1_HD // 2, -1.0, 1.0).astype(np.float32)
    t["l1_cos"], t["l1_sin"] = by_tile(np.cos(f)), by_tile(np.sin(f) * sign)
    f, half = rotary_angles(SEQ, LOC_HD, np)
    base = (half + np.float32(0.4 * LOC_HD)) / np.float32(1.4 * LOC_HD)
    power = (np.arange(SEQ, dtype=np.float32) - SEQ // 2) / np.float32(WINDOW // 2)
    scale = np.power(base[None, :], power[:, None]).astype(np.float32)
    scale = np.concatenate([scale, scale], -1)
    inv = (np.float32(1.0) / scale).astype(np.float32)
    sign = np.where(np.arange(LOC_HD) < LOC_HD // 2, -1.0, 1.0).astype(np.float32)
    c, s = np.cos(f), np.sin(f) * sign
    t["lo_rotary"] = np.stack([by_tile(x) for x in (c * scale, s * scale, c * inv, s * inv)], 1)
    i = np.arange(P)[:, None]
    t["mask0"] = np.where(np.arange(P)[None, :] > i, L0_MASK, 0.0)
    j = np.arange(LOC_KEYS)[None, :] - WINDOW
    hidden = (j > i) | (j < i - WINDOW)
    mask = np.stack([hidden | (j < 0)] + [hidden] * (TILES - 1), 1)
    t["lo_mask"] = np.where(mask, -1e30, 0.0)
    t["lo_shift"] = np.stack([np.eye(P, k=1), np.eye(P, k=1 - P)], 1)
    t["ident"] = np.eye(P)
    t = {k: np.ascontiguousarray(v, dtype=np.float32) for k, v in t.items()}
    for k in ("mask0", "lo_mask"):
        t[k] = t[k].astype(mybir.dt.np(BF16))
    return t


def kernel(**x):
    import numpy as np
    import concourse.bacc as bacc
    from concourse.bass_utils import run_bass_kernel_spmd

    x = {k: np.asarray(v) for k, v in x.items()}
    flat = lambda w: w.reshape(HEADS * L0_HD, DIM).T
    arrays = {
        "x": x["L0_attn_x"].reshape(BATCH * SEQ, DIM),
        "l0_w": np.stack([flat(x["L0_attn_W_K"]), flat(x["L0_attn_W_Q"]), flat(x["L0_attn_W_V"])]),
        "l0_wo": x["L0_attn_W_O"].transpose(0, 2, 1).reshape(HEADS * L0_HD, DIM),
        "w8T": x["L0_ffn_weight"].T, "bias0": x["L0_ffn_bias"],
        "l1_w": x["L1_attn_w_qkv"].T, "l1_wo": x["L1_attn_w_out"].T, "b_out": x["L1_attn_b_out"],
        "Wqkv": x["L1_ffn_Wqkv"], "Wo": x["L1_ffn_Wo"], "W1": x["L1_ffn_W1"], "W2": x["L1_ffn_W2"],
        "b1": x["L1_ffn_b1"], "b2": x["L1_ffn_b2"],
        "ln": np.stack([x["L1_ffn_ln_g"].T, x["L1_ffn_ln_b"].T], -1),
    }
    q, k = x["L1_ffn_q_scale"], x["L1_ffn_k_scale"]
    swap = lambda s: np.concatenate([s[:, LOC_HD // 2:], s[:, :LOC_HD // 2]], -1)
    arrays["lo_scales"] = np.stack([q, swap(q), k, swap(k)], 1)
    arrays.update(shape_tables(np))
    nc = bacc.Bacc("TRN2", target_bir_lowering=False, num_devices=1)
    dram = {}
    for name, value in arrays.items():
        arrays[name] = np.ascontiguousarray(value)
        dram[name] = nc.dram_tensor(f"in_{name}", arrays[name].shape, mybir.dt.from_np(arrays[name].dtype), kind="ExternalInput").ap()
    out = nc.dram_tensor("out", (BATCH, SEQ, DIM), F32, kind="ExternalOutput").ap()
    build(nc, dram, out)
    r = run_bass_kernel_spmd(nc, [{f"in_{k}": v for k, v in arrays.items()}], core_ids=[0])
    return r.results[0]["out"]
```

```python
from contextlib import ExitStack

import concourse.bass as bass
from concourse import mybir

F32 = mybir.dt.float32
BF16 = mybir.dt.bfloat16
F16 = mybir.dt.float16
FP8 = mybir.dt.float8e4
ALU = mybir.AluOpType
ACT = mybir.ActivationFunctionType
AX = mybir.AxisListType

P = 128
BATCH, SEQ, DIM = 4, 1024, 128
TILES = SEQ // P
ALL_TILES = BATCH * TILES
HEADS = 16
PAIRS = HEADS // 2
LN_EPS = 1e-5

L0_HD = 64
L1_HD = DIM // HEADS
SPLIT = 3
L0_MASK = -1e10

DEPTH = 6
LOC_HD = 64
WINDOW = 32
INNER = HEADS * LOC_HD
DIM_INNER = int(DIM * 4 * 2 / 3)
QK_SCALE = 8.0
LOC_KEYS = WINDOW + P
GROUP = 4
GROUPS = HEADS // GROUP
VW = LOC_HD + 1


class Mem:

    def __init__(self, nc, ctx):
        self.nc, self.ctx = nc, ctx

    def sb(self, name, shape, dt=F32):
        return self.ctx.enter_context(self.nc.sbuf_tensor(name, shape, dt))

    def ps(self, name, shape, dt=F32):
        return self.ctx.enter_context(self.nc.psum_tensor(name, shape, dt))

    def sem(self, name):
        return self.ctx.enter_context(self.nc.semaphore(name))


def load_phase(nc, keep, dram):
    with ExitStack() as ctx:
        m = Mem(nc, ctx)
        w = m.sb("w8_raw", [P, P])
        small = m.sb("w8_small", [P, P])
        large = m.sb("w8_large", [P, P])
        small8 = m.sb("w8_small8", [P, P], FP8)
        large8 = m.sb("w8_large8", [P, P], FP8)
        small_r = m.sb("w8_small_r", [P, P])
        large_r = m.sb("w8_large_r", [P, P])
        mag = m.sb("w8_mag", [P, P])
        is_large = m.sb("w8_is_large", [P, P])
        is_small = m.sb("w8_is_small", [P, P])
        loaded = m.sem("loaded")
        step = m.sem("w8_step")
        zeroed = m.sem("zeroed")
        with nc.Block() as block:

            @block.sync
            def _(sp):
                sp.dma_start(keep.xres[:], dram["x"].rearrange("(t p) c -> p t c", p=P)).then_inc(loaded, 16)
                sp.dma_start(w[:], dram["w8T"]).then_inc(loaded, 16)
                sp.dma_start(keep.ident[:], dram["ident"]).then_inc(loaded, 16)
                sp.dma_start(keep.bias0[:], dram["bias0"].rearrange("(a c) -> a c", a=1).broadcast_to([P, P])).then_inc(loaded, 16)
                sp.dma_start(keep.bias1[:], dram["b_out"].rearrange("(a c) -> a c", a=1).broadcast_to([P, P])).then_inc(loaded, 16)
                sp.wait_ge(loaded, 80)

            @block.gpsimd
            def _(pool):
                pool.memset(keep.y_in[:], 0.0).then_inc(zeroed, 1)
                pool.memset(keep.y_mid[:], 0.0).then_inc(zeroed, 1)
                pool.memset(keep.neg_half[:], -0.5).then_inc(zeroed, 1)
                pool.wait_ge(zeroed, 3)

            @block.vector
            def _(dve):
                dve.wait_ge(loaded, 80)
                dve.tensor_copy(keep.identb[:], keep.ident[:]).then_inc(step, 1)
                dve.tensor_scalar(small[:], w[:], 128.0, -128.0, ALU.min, ALU.max).then_inc(step, 1)
                dve.tensor_scalar(large[:], w[:], 448.0, -448.0, ALU.min, ALU.max).then_inc(step, 1)
                dve.wait_ge(step, 3)
                dve.tensor_copy(small8[:], small[:], saturate=False).then_inc(step, 1)
                dve.tensor_scalar(large8[:], large[:], 0.5, None, ALU.mult, saturate=False).then_inc(step, 1)
                dve.tensor_scalar(mag[:], large[:], -1.0, None, ALU.mult).then_inc(step, 1)
                dve.wait_ge(step, 6)
                dve.tensor_tensor(is_small[:], mag[:], large[:], ALU.max).then_inc(step, 1)
                dve.wait_ge(step, 7)
                dve.tensor_scalar(is_large[:], is_small[:], 128.0, 2.0, ALU.is_gt, ALU.mult).then_inc(step, 1)
                dve.wait_ge(step, 8)
                dve.tensor_scalar(is_small[:], is_large[:], -0.5, 1.0, ALU.mult, ALU.add).then_inc(step, 1)
                dve.wait_ge(step, 9)
                dve.tensor_tensor(small_r[:], small8[:], is_small[:], ALU.mult).then_inc(step, 1)
                dve.tensor_tensor(large_r[:], large8[:], is_large[:], ALU.mult).then_inc(step, 1)
                dve.wait_ge(step, 11)
                dve.tensor_tensor(keep.w8[:], small_r[:], large_r[:], ALU.add).then_inc(step, 1)
                dve.wait_ge(step, 12)


NT = 4
NORM_STEPS = ALL_TILES // NT


def norm0_phase(nc, keep):
    with ExitStack() as ctx:
        m = Mem(nc, ctx)
        stats = m.sb("n0_stats", [P, NT, 6])
        meanvar = m.sb("n0_meanvar", [P, NT, 2])
        var = m.sb("n0_var", [P, NT])
        rstd = m.sb("n0_rstd", [P, NT])
        xn = m.sb("n0_xn", [P, NT, P])
        x8 = m.sb("n0_x8", [P, NT * P], FP8)
        x8b = m.sb("n0_x8b", [P, NT * P], BF16)
        y16 = m.sb("n0_y16", [P, NT, P], F16)
        xbias = m.sb("n0_xbias", [P, NT, P])
        ps_t = m.ps("n0_ps_t", [P, NT * P])
        ps_y = m.ps("n0_ps_y", [P, NT, P])
        stats_done, var_done, rstd_done = m.sem("n0_stats_done"), m.sem("n0_var_done"), m.sem("n0_rstd_done")
        var_eps = m.sem("n0_var_eps")
        xn_done, transposed, xnT_done = m.sem("n0_xn_done"), m.sem("n0_transposed"), m.sem("n0_xnT_done")
        x8_done, x8b_done, mm_done, y16_done = m.sem("n0_x8_done"), m.sem("n0_x8b_done"), m.sem("n0_mm_done"), m.sem("n0_y16_done")
        bias_done, x_done = m.sem("n0_bias_done"), m.sem("n0_x_done")
        with nc.Block() as block:

            @block.vector
            def _(dve):
                dve.sem_inc(y16_done, 1)
                dve.sem_inc(x_done, 1)

                def statistics(g):
                    for j in range(NT):
                        dve.bn_stats(stats[:, j, :], keep.xres[:, bass.ds(g * NT + j, 1), :].rearrange("p a c -> p (a c)")).then_inc(stats_done, 1)
                    dve.wait_ge(stats_done, g * NT + NT)
                    dve.nop(nofuse=True)
                    for j in range(NT):
                        dve.bn_aggr(meanvar[:, j, :], stats[:, j, :]).then_inc(var_done, 1)

                def normalize(g, last):
                    dve.wait_ge(rstd_done, g + 1)
                    for j in range(NT):
                        dve.tensor_scalar(xn[:, j, :], keep.xres[:, bass.ds(g * NT + j, 1), :].rearrange("p a c -> p (a c)"),
                                          meanvar[:, j, 0:1], rstd[:, j:j + 1], ALU.subtract, ALU.mult).then_inc(xn_done, 1)
                    if not last:
                        statistics(g + 1)
                    dve.wait_ge(xnT_done, g + 1)
                    dve.nop(nofuse=True)
                    dve.tensor_copy(x8[:], ps_t[:], saturate=False).then_inc(x8_done, 1)
                    dve.wait_ge(x8_done, g + 1)
                    dve.nop(nofuse=True)
                    dve.tensor_copy(x8b[:], x8[:]).then_inc(x8b_done, 1)
                    dve.wait_ge(mm_done, g + 1)
                    dve.tensor_copy(y16[:], ps_y[:]).then_inc(y16_done, 1)
                    dve.wait_ge(y16_done, g + 2)
                    dve.wait_ge(bias_done, g + 1)
                    dve.tensor_tensor(keep.xres[:, bass.ds(g * NT, NT), :], y16[:], xbias[:], ALU.add).then_inc(x_done, 1)

                statistics(0)
                with dve.Fori(0, NORM_STEPS - 1) as g:
                    normalize(g, False)
                normalize(NORM_STEPS - 1, True)

            @block.gpsimd
            def _(pool):
                with pool.Fori(0, NORM_STEPS) as g:
                    pool.wait_ge(var_done, g * NT + NT)
                    pool.nop(nofuse=True)
                    pool.tensor_scalar(var[:], meanvar[:, :, 1], LN_EPS, None, ALU.add).then_inc(var_eps, 1)
                    pool.wait_ge(var_eps, g + 1)
                    pool.tensor_tensor(rstd[:], var[:], keep.neg_half[:, 0:NT], ALU.pow).then_inc(rstd_done, 1)
                    pool.wait_ge(x_done, g + 1)
                    pool.nop(nofuse=True)
                    pool.tensor_tensor(xbias[:], keep.xres[:, bass.ds(g * NT, NT), :],
                                       keep.bias0[:].rearrange("p (a c) -> p a c", a=1).broadcast_to([P, NT, P]), ALU.add).then_inc(bias_done, 1)

            @block.tensor
            def _(pe):
                with pe.Fori(0, NORM_STEPS) as g:
                    pe.wait_ge(xn_done, g * NT + NT)
                    for j in range(NT):
                        last = pe.transpose(ps_t[:, j * P:(j + 1) * P], xn[:, j, :], keep.ident[:])
                    last.then_inc(transposed, 1)
                    pe.wait_ge(x8b_done, g + 1)
                    pe.wait_ge(y16_done, g + 1)
                    for j in range(NT):
                        last = pe.matmul(ps_y[:, j, :], x8b[:, j * P:(j + 1) * P], keep.w8[:], start=True, stop=True)
                    last.then_inc(mm_done, 1)

            @block.scalar
            def _(act):
                with act.Fori(0, NORM_STEPS) as g:
                    act.wait_ge(transposed, g + 1)
                    act.copy(keep.xnT[:, bass.ds(g * NT * P, NT * P)], ps_t[:]).then_inc(xnT_done, 1)


def causal_attention_phase(nc, keep):
    vd = L0_HD
    scale = 1.0 / float(vd) ** 0.5
    width = HEADS * vd
    chunks = width // P
    UNITS = 4 * TILES
    PREP = 6
    units = [(pl, h, t) for pl in range(2) for h in range(2) for t in range(TILES)]
    blocks = [t + 1 for _, _, t in units]
    second = [n > 4 for n in blocks]
    n_second = sum(second)
    second_at = [sum(second[:u]) for u in range(UNITS)]
    prep_at = {16 * pl + 5 + c: (pl, c) for pl in range(2) for c in range(PREP)}

    with ExitStack() as ctx:
        m = Mem(nc, ctx)
        rowT = [m.sb(f"ca_rowT{s}", [P, 2, SEQ]) for s in range(2)]
        colT = [m.sb(f"ca_colT{s}", [P, SEQ]) for s in range(2)]
        val = [m.sb(f"ca_val{s}", [P, TILES, 2 * vd]) for s in range(2)]
        prob = m.sb("ca_prob", [P, 2, SEQ])
        probT = m.sb(f"ca_probT", [P, 2, TILES, P])
        neg_max = m.sb("ca_neg_max", [P, 4])
        row_max = m.sb("ca_row_max", [P, 4])
        den = m.sb("ca_den", [P, 4])
        rden = m.sb("ca_rden", [P, 4])
        zn = m.sb("ca_zn", [P, TILES, width])
        wqkv = m.sb("ca_wqkv", [P, 3, width])
        wstage = m.sb("ca_wstage", [P, 3, P])
        xstage = m.sb("ca_xstage", [P, SEQ])
        wout = m.sb("ca_wout", [P, chunks, P])
        mask = m.sb("ca_mask", [P, P], BF16)
        ps_s = m.ps("ca_ps_s", [P, 2, SEQ])
        ps_t = m.ps("ca_ps_t", [P, 2, 4, P])
        ps_z = m.ps("ca_ps_z", [P, 512])
        ps_m = m.ps("ca_ps_m", [P, 512])
        w_loaded, rows_cleared = m.sem("ca_w_loaded"), m.sem("ca_rows_cleared")
        staged, prep_mm, prep_copied = m.sem("ca_staged"), m.sem("ca_prep_mm"), m.sem("ca_prep_copied")
        scored, max_done, negmax_done, exp_done = (m.sem("ca_" + x) for x in ("scored", "max_done", "negmax_done", "exp_done"))
        t_bank = [m.sem(f"ca_t_bank{k}") for k in range(2)]
        copied = [m.sem(f"ca_copied{k}") for k in range(2)]
        pv_done, rden_done, z_done = m.sem("ca_pv_done"), m.sem("ca_rden_done"), m.sem("ca_z_done")
        o_t = [m.sem(f"ca_o_t{k}") for k in range(2)]
        o_c = [m.sem(f"ca_o_c{k}") for k in range(2)]
        o_mm, o_add = m.sem("ca_o_mm"), m.sem("ca_o_add")
        PER_B = 4

        with nc.Block() as block:

            @block.sync
            def _(sp):
                for k in range(3):
                    sp.dma_start(wqkv[:, k, :], keep.dram["l0_w"][k]).then_inc(w_loaded, 16)
                sp.dma_start(mask[:], keep.dram["mask0"]).then_inc(w_loaded, 16)
                sp.dma_start(wout[:], keep.dram["l0_wo"].rearrange("(k p) e -> p k e", p=P)).then_inc(w_loaded, 16)
                sp.wait_ge(w_loaded, 80)

            @block.gpsimd
            def _(pool):
                pool.wait_ge(w_loaded, 80)
                for s in range(2):
                    pool.memset(rowT[s][:], 0.0).then_inc(rows_cleared, 1)

                def stage_pair(n1):
                    w = n1 & (PAIRS - 1)
                    b = (n1 >> 3) & (BATCH - 1)
                    pool.wait_ge(prep_mm, n1 * PREP + 1)
                    pool.nop(nofuse=True)
                    pool.tensor_copy(wstage[:], wqkv[:, :, bass.ds(w * P, P)]).then_inc(staged, 1)
                    pool.tensor_copy(xstage[:], keep.xnT[:, bass.ds(b * SEQ, SEQ)]).then_inc(staged, 1)

                pool.sem_inc(prep_mm, 1)
                stage_pair(0)
                with pool.Fori(0, BATCH * PER_B) as i:
                    for pl in range(2):
                        stage_pair(2 * i + pl + 1)

                pool.wait_ge(staged, 2 * (2 * BATCH * PER_B + 1))

            @block.tensor
            def _(pe):
                def prepare(n1, c, slot):
                    pe.wait_ge(prep_copied, n1 * PREP + c + 1)
                    pe.wait_ge(staged, 2 * n1 + 2)
                    if c < 4:
                        last = pe.matmul(ps_m[:], wstage[:, c // 2, :], xstage[:, (c % 2) * 512:(c % 2 + 1) * 512], start=True, stop=True)
                    else:
                        for j in range(4):
                            t = 4 * (c - 4) + j
                            last = pe.matmul(ps_m[:, j * P:(j + 1) * P], xstage[:, t * P:(t + 1) * P], wstage[:, 2, :], start=True, stop=True)
                    last.then_inc(prep_mm, 1)

                def scores(i, u):
                    pl, h, t = units[u]
                    n = blocks[u] * P
                    if h == 0 and t == 0:
                        pe.wait_ge(prep_copied, (2 * i + pl + 1) * PREP + 1)
                    pe.wait_ge(exp_done, i * UNITS + u + 1)
                    for k in range(0, n, 512):
                        e = min(n, k + 512)
                        diag = t * P >= k and t * P < e
                        last = pe.matmul(ps_s[:, u % 2, k:e], rowT[pl][:, h, t * P:(t + 1) * P],
                                         colT[pl][:, k:e], start=True, stop=not diag)
                        if diag:
                            last = pe.matmul(ps_s[:, u % 2, t * P:(t + 1) * P], keep.identb[:], mask[:], start=False, stop=True)
                    last.then_inc(scored, 1)

                def transposes(i, u):
                    pe.wait_ge(exp_done, i * UNITS + u + 3)
                    for j in range(blocks[u]):
                        k = j // 4
                        if j == 0:
                            pe.wait_ge(copied[0], i * UNITS + u + 1)
                        if j == 4:
                            pe.wait_ge(copied[1], i * n_second + second_at[u] + 1)
                        last = pe.transpose(ps_t[:, k, j % 4, :], prob[:, u % 2, j * P:(j + 1) * P], keep.ident[:])
                        if j == 3 and blocks[u] > 4:
                            last.then_inc(t_bank[0], 1)
                    if blocks[u] <= 4:
                        last.then_inc(t_bank[0], 1)
                    else:
                        last.then_inc(t_bank[1], 1)

                def values(i, u):
                    pl, h, t = units[u]
                    pe.wait_ge(copied[0], i * UNITS + u + 2)
                    if second[u]:
                        pe.wait_ge(copied[1], i * n_second + second_at[u] + 2)
                    pe.wait_ge(z_done, i * UNITS + u + 1)
                    for j in range(blocks[u]):
                        last = pe.matmul(ps_z[:, 0:vd], probT[:, u % 2, j, :], val[pl][:, j, h * vd:(h + 1) * vd],
                                         start=(j == 0), stop=(j == blocks[u] - 1))
                    last.then_inc(pv_done, 1)

                def project(b):
                    pe.wait_ge(z_done, (b + 1) * PER_B * UNITS + 1)
                    for t in range(TILES + 1):
                        if t < TILES:
                            for k in range(2):
                                if t > 0:
                                    pe.wait_ge(o_c[k], b * TILES + t)
                                for j in range(4):
                                    last = pe.transpose(ps_t[:, k, j, :], zn[:, t, (4 * k + j) * P:(4 * k + j + 1) * P], keep.ident[:])
                                last.then_inc(o_t[k], 1)
                        if t == 0:
                            continue
                        pe.wait_ge(o_add, b * TILES + t)
                        for k in range(2):
                            pe.wait_ge(o_c[k], b * TILES + t)
                            for j in range(4):
                                c = 4 * k + j
                                last = pe.matmul(ps_z[:, 0:P], probT[:, (t - 1) % 2, c, :], wout[:, c, :], start=(c == 0), stop=(c == chunks - 1))
                        last.then_inc(o_mm, 1)
                    pe.wait_ge(o_add, (b + 1) * TILES + 1)

                pe.wait_ge(w_loaded, 80)
                for c in range(PREP):
                    prepare(0, c, 0)
                with pe.Fori(0, BATCH) as b:
                    with pe.Fori(0, PER_B) as ii:
                        i = b * PER_B + ii
                        for s in range(UNITS + 3):
                            if s < UNITS:
                                scores(i, s)
                            if s in prep_at:
                                pl, c = prep_at[s]
                                prepare(2 * i + pl + 1, c, (pl + 1) % 2)
                            if 2 <= s < UNITS + 2:
                                transposes(i, s - 2)
                            if s >= 3:
                                values(i, s - 3)
                    project(b)

            @block.vector
            def _(dve):
                dve.wait_ge(w_loaded, 80)
                dve.sem_inc(copied[1], 1)
                dve.sem_inc(z_done, 1)
                dve.sem_inc(o_add, 1)

                def maximum(i, u):
                    dve.wait_ge(scored, i * UNITS + u + 1)
                    dve.wait_ge(exp_done, i * UNITS + u + 1)
                    dve.tensor_reduce(row_max[:, u % 2:u % 2 + 1], ps_s[:, u % 2, 0:blocks[u] * P], AX.X, ALU.max).then_inc(max_done, 1)
                    dve.wait_ge(max_done, i * UNITS + u + 1)
                    dve.tensor_scalar(neg_max[:, u % 2:u % 2 + 1], row_max[:, u % 2:u % 2 + 1], -scale, None, ALU.mult).then_inc(negmax_done, 1)

                def copy_second(i, u):
                    dve.wait_ge(t_bank[1], i * n_second + second_at[u] + 1)
                    dve.wait_ge(pv_done, i * UNITS + u + 1)
                    dve.tensor_copy(probT[:, u % 2, 4:blocks[u], :], ps_t[:, 1, 0:blocks[u] - 4, :]).then_inc(copied[1], 1)

                def normalize(i, b, ii, u):
                    pl, h, t = units[u]
                    dve.wait_ge(pv_done, i * UNITS + u + 3)
                    dve.reciprocal(rden[:, 0:1], den[:, u % 4:u % 4 + 1]).then_inc(rden_done, 1)
                    dve.wait_ge(rden_done, i * UNITS + u + 1)
                    dve.tensor_scalar(zn[:, t, bass.ds(ii * 4 * vd + (2 * pl + h) * vd, vd)], ps_z[:, 0:vd], rden[:, 0:1], None,
                                      ALU.mult).then_inc(z_done, 1)

                def copy_values(n1, c, slot):
                    dve.wait_ge(prep_mm, n1 * PREP + c + 2)
                    dve.tensor_copy(val[slot][:, 4 * (c - 4):4 * (c - 3), :], ps_m[:].rearrange("p (t d) -> p t d", t=4)).then_inc(prep_copied, 1)

                for c in (4, 5):
                    copy_values(0, c, 0)
                with dve.Fori(0, BATCH) as b:
                    with dve.Fori(0, PER_B) as ii:
                        i = b * PER_B + ii
                        for s in range(UNITS + 3):
                            if s < UNITS:
                                maximum(i, s)
                            if 2 <= s < UNITS + 2 and second[s - 2]:
                                copy_second(i, s - 2)
                            if s in prep_at and prep_at[s][1] >= 4:
                                pl, c = prep_at[s]
                                copy_values(2 * i + pl + 1, c, (pl + 1) % 2)
                            if s >= 3:
                                normalize(i, b, ii, s - 3)
                    for t in range(TILES + 1):
                        if t < TILES:
                            dve.wait_ge(o_t[1], b * TILES + t + 1)
                            dve.wait_ge(o_add, b * TILES + max(t, 1))
                            dve.tensor_copy(probT[:, t % 2, 4:8, :], ps_t[:, 1, :, :]).then_inc(o_c[1], 1)
                        if t == 0:
                            continue
                        dve.wait_ge(o_mm, b * TILES + t)
                        row = keep.xres[:, bass.ds(b * TILES + t - 1, 1), :].rearrange("p a c -> p (a c)")
                        dve.tensor_tensor(row, ps_z[:, 0:P], row, ALU.add).then_inc(o_add, 1)

            @block.scalar
            def _(act):
                act.sem_inc(exp_done, 2)
                act.sem_inc(pv_done, 2)
                act.sem_inc(copied[0], 1)
                act.sem_inc(prep_copied, 1)

                def exponentials(i, u):
                    act.wait_ge(negmax_done, i * UNITS + u + 1)
                    act.activation(prob[:, u % 2, 0:blocks[u] * P], ps_s[:, u % 2, 0:blocks[u] * P], ACT.Exp,
                                   bias=neg_max[:, u % 2:u % 2 + 1], scale=scale, accum_out=den[:, u % 4:u % 4 + 1]).then_inc(exp_done, 1)

                def copy_first(i, u):
                    act.wait_ge(t_bank[0], i * UNITS + u + 1)
                    act.wait_ge(pv_done, i * UNITS + u + 1)
                    n = min(4, blocks[u])
                    act.copy(probT[:, u % 2, 0:n, :], ps_t[:, 0, 0:n, :]).then_inc(copied[0], 1)

                def copy_operand(n1, c, slot):
                    act.wait_ge(prep_mm, n1 * PREP + c + 2)
                    cols = slice((c % 2) * 512, (c % 2 + 1) * 512)
                    if c < 2:
                        act.copy(rowT[slot][0:64, 0, cols], ps_m[0:64])
                        act.copy(rowT[slot][64:128, 1, cols], ps_m[64:128]).then_inc(prep_copied, 1)
                    else:
                        act.copy(colT[slot][:, cols], ps_m[:]).then_inc(prep_copied, 1)

                act.wait_ge(rows_cleared, 2)
                for c in range(4):
                    copy_operand(0, c, 0)
                with act.Fori(0, BATCH) as b:
                    with act.Fori(0, PER_B) as ii:
                        i = b * PER_B + ii
                        for s in range(UNITS + 3):
                            if 1 <= s < UNITS + 1:
                                if s >= 3:
                                    act.wait_ge(t_bank[1] if second[s - 3] else t_bank[0],
                                                i * n_second + second_at[s - 3] + 1 if second[s - 3] else i * UNITS + s - 2)
                                exponentials(i, s - 1)
                            if 2 <= s < UNITS + 2:
                                copy_first(i, s - 2)
                            if s in prep_at and prep_at[s][1] < 4:
                                pl, c = prep_at[s]
                                copy_operand(2 * i + pl + 1, c, (pl + 1) % 2)
                    for t in range(TILES):
                        act.wait_ge(o_t[0], b * TILES + t + 1)
                        act.wait_ge(o_add, b * TILES + max(t, 1))
                        act.copy(probT[:, t % 2, 0:4, :], ps_t[:, 0, 0:4, :]).then_inc(o_c[0], 1)


def norm1_phase(nc, keep):
    SH = 2 * HEADS
    with ExitStack() as ctx:
        m = Mem(nc, ctx)
        stats = m.sb("n1_stats", [P, NT, 6])
        meanvar = m.sb("n1_meanvar", [P, NT, 2])
        var = m.sb("n1_var", [P, NT])
        rstd = m.sb("n1_rstd", [P, NT])
        xn = m.sb("n1_xn", [P, NT, P])
        xT = m.sb("n1_xT", [P, NT * P])
        wqkv = m.sb("n1_wqkv", [P, 3 * DIM])
        cos = m.sb("n1_cos", [P, TILES, L1_HD])
        sin = m.sb("n1_sin", [P, TILES, L1_HD])
        qk = m.sb("n1_qk", [P, NT, SH, L1_HD])
        by_cos = m.sb("n1_by_cos", [P, NT, SH, L1_HD])
        by_sin = m.sb("n1_by_sin", [P, NT, SH, L1_HD])
        rot = m.sb("n1_rot", [P, NT, SH, L1_HD])
        rest1 = m.sb("n1_rest1", [P, NT, SH, L1_HD])
        rest2 = m.sb("n1_rest2", [P, NT, SH, L1_HD])
        ps_t = m.ps("n1_ps_t", [P, NT * P])
        ps_q = m.ps("n1_ps_q", [P, NT, 512])
        loaded = m.sem("n1_loaded")
        stats_done, var_done, var_eps, rstd_done = (m.sem("n1_" + x) for x in ("stats_done", "var_done", "var_eps", "rstd_done"))
        xn_done, transposed, xT_done, mm_done = (m.sem("n1_" + x) for x in ("xn_done", "transposed", "xT_done", "mm_done"))
        qk_done, step, y_done = m.sem("n1_qk_done"), m.sem("n1_step"), m.sem("n1_y_done")
        STEPS = 9
        with nc.Block() as block:

            @block.sync
            def _(sp):
                sp.dma_start(wqkv[:], keep.dram["l1_w"]).then_inc(loaded, 16)
                sp.dma_start(cos[:], keep.dram["l1_cos"]).then_inc(loaded, 16)
                sp.dma_start(sin[:], keep.dram["l1_sin"]).then_inc(loaded, 16)
                sp.wait_ge(loaded, 48)

            @block.vector
            def _(dve):
                dve.wait_ge(loaded, 48)
                dve.sem_inc(step, 1)
                def statistics(g):
                    for j in range(NT):
                        dve.bn_stats(stats[:, j, :], keep.xres[:, bass.ds(g * NT + j, 1), :].rearrange("p a c -> p (a c)")).then_inc(stats_done, 1)
                    dve.wait_ge(stats_done, g * NT + NT)
                    dve.nop(nofuse=True)
                    for j in range(NT):
                        dve.bn_aggr(meanvar[:, j, :], stats[:, j, :]).then_inc(var_done, 1)

                def normalize(g, last):
                    dve.wait_ge(rstd_done, g + 1)
                    dve.wait_ge(y_done, g + 1)
                    for j in range(NT):
                        dve.tensor_scalar(xn[:, j, :], keep.xres[:, bass.ds(g * NT + j, 1), :].rearrange("p a c -> p (a c)"),
                                          meanvar[:, j, 0:1], rstd[:, j:j + 1], ALU.subtract, ALU.mult).then_inc(xn_done, 1)
                    if not last:
                        statistics(g + 1)
                    half = L1_HD // 2
                    t0 = (g & 1) * NT

                    def table(tab, lo, hi):
                        return tab[:, bass.ds(t0, NT), lo:hi].rearrange("p t (a d) -> p t a d", a=1).broadcast_to([P, NT, SH, hi - lo])

                    def own(n):
                        dve.wait_ge(step, g * STEPS + n + 1)

                    dve.wait_ge(qk_done, g + 1)
                    odd_even = qk[:].rearrange("p t h (d two) -> p t h d two", two=2)
                    dve.tensor_tensor(by_cos[:], qk[:], table(cos, 0, L1_HD), ALU.mult).then_inc(step, 1)
                    dve.tensor_tensor(by_sin[:, :, :, 0:half], odd_even[:, :, :, :, 1], table(sin, 0, half), ALU.mult).then_inc(step, 1)
                    dve.tensor_tensor(by_sin[:, :, :, half:], odd_even[:, :, :, :, 0], table(sin, half, L1_HD), ALU.mult).then_inc(step, 1)
                    own(3)
                    dve.tensor_tensor(rot[:], by_cos[:], by_sin[:], ALU.add).then_inc(step, 1)
                    own(4)

                    def part(k):
                        return keep.qk3[:, bass.ds(g * NT, NT), k, :, :]

                    dve.tensor_copy(part(0), rot[:]).then_inc(step, 1)
                    own(5)
                    dve.tensor_tensor(rest1[:], rot[:], part(0), ALU.subtract).then_inc(step, 1)
                    own(6)
                    dve.tensor_copy(part(1), rest1[:]).then_inc(step, 1)
                    own(7)
                    dve.tensor_tensor(rest2[:], rest1[:], part(1), ALU.subtract).then_inc(step, 1)
                    own(8)
                    dve.tensor_copy(part(2), rest2[:]).then_inc(step, 1)

                statistics(0)
                with dve.Fori(0, NORM_STEPS - 1) as g:
                    normalize(g, False)
                normalize(NORM_STEPS - 1, True)

            @block.gpsimd
            def _(pool):
                pool.sem_inc(y_done, 1)
                with pool.Fori(0, NORM_STEPS) as g:
                    pool.wait_ge(var_done, g * NT + NT)
                    pool.nop(nofuse=True)
                    pool.tensor_scalar(var[:], meanvar[:, :, 1], LN_EPS, None, ALU.add).then_inc(var_eps, 1)
                    pool.wait_ge(var_eps, g + 1)
                    pool.tensor_tensor(rstd[:], var[:], keep.neg_half[:, 0:NT], ALU.pow).then_inc(rstd_done, 1)
                    pool.wait_ge(xn_done, g * NT + NT)
                    pool.nop(nofuse=True)
                    pool.tensor_copy(keep.y_in[:, bass.ds(g * NT + (g >> 1) + 1, NT), :], xn[:]).then_inc(y_done, 1)

            @block.tensor
            def _(pe):
                pe.wait_ge(loaded, 48)
                with pe.Fori(0, NORM_STEPS) as g:
                    pe.wait_ge(xn_done, g * NT + NT)
                    for j in range(NT):
                        last = pe.transpose(ps_t[:, j * P:(j + 1) * P], xn[:, j, :], keep.ident[:])
                    last.then_inc(transposed, 1)
                    pe.wait_ge(xT_done, g + 1)
                    for j in range(NT):
                        last = pe.matmul(ps_q[:, j, 0:3 * DIM], xT[:, j * P:(j + 1) * P], wqkv[:], start=True, stop=True)
                    last.then_inc(mm_done, 1)

            @block.scalar
            def _(act):
                with act.Fori(0, NORM_STEPS) as g:
                    act.wait_ge(transposed, g + 1)
                    act.copy(xT[:], ps_t[:]).then_inc(xT_done, 1)
                    act.wait_ge(mm_done, g + 1)
                    act.wait_ge(step, g * STEPS + 1)
                    act.copy(keep.v1[:, bass.ds(g * NT, NT), :, :].rearrange("p t h d -> p t (h d)"), ps_q[:, :, 2 * DIM:3 * DIM])
                    act.copy(qk[:].rearrange("p t h d -> p t (h d)"), ps_q[:, :, 0:2 * DIM]).then_inc(qk_done, 1)


class Keep:
    pass


def full_attention_phase(nc, keep):
    QUAD = 4
    QUADS = HEADS // QUAD
    N = BATCH * QUADS
    ROWS = 64
    MAX_ROW = 32
    HALF_SEQ = SEQ // 2
    VC = 32
    scale = 1.0 / float(L1_HD) ** 0.5
    ST = 2 * TILES * 2
    FIRST = QUAD * TILES * 2
    PARTS = ((0, (0, 0), (0, 0)), (1, (0, 1), (8, 8)), (2, (1, 0), (16, 16)), (3, (1, 1), (24, 24)),
             (4, (0, 2), (40, 40)), (5, (2, 0), (48, 48)))
    STAGED = 2 * len(PARTS)
    first_until = [min(FIRST, max(0, round((s - 2) * FIRST / 26))) for s in range(ST)]

    with ExitStack() as ctx:
        m = Mem(nc, ctx)
        stage = m.sb("fa_stage", [P, 2, TILES, QUAD, ROWS], BF16)
        rowT = [m.sb(f"fa_rowT{s}", [P, QUAD, SEQ], BF16) for s in range(2)]
        colT = [m.sb(f"fa_colT{s}", [P, 2, SEQ], BF16) for s in range(2)]
        val = [m.sb(f"fa_val{s}", [P, TILES, QUAD, VC]) for s in range(2)]
        row_max = m.sb("fa_row_max", [P, QUAD, TILES, 2])
        max_of = m.sb("fa_max_of", [P, QUAD, TILES])
        max_parts = m.sb("fa_max_parts", [P, QUAD, TILES, 2], BF16)
        prob = m.sb("fa_prob", [P, 2, QUAD, HALF_SEQ])
        zT = m.sb("fa_zT", [P, 2, HALF_SEQ])
        rden = m.sb("fa_rden", [P, QUAD, QUAD])
        zn = m.sb("fa_zn", [P, ALL_TILES, DIM])
        slab = prob[:].rearrange("p s h k -> p s (h k)")[:, :, 0:TILES * DIM].rearrange("p s (t c) -> p s t c", c=DIM)
        znT = m.sb("fa_znT", [P, 2, HALF_SEQ])
        wout = m.sb("fa_wout", [P, DIM])
        ps = m.ps("fa_ps", [P, 8, 512])
        S1, STB, MISC, ZB = 0, 2, 6, 7
        miscb = ps[:, MISC, :].bitcast(BF16)
        sem = lambda name: m.sem("fa_" + name)
        w_loaded, biased, cleared, staged, val_staged, rows_cleared = sem("w_loaded"), sem("biased"), sem("cleared"), sem("staged"), sem("val_staged"), sem("rows_cleared")
        prep_filled, row_copied, col_copied = sem("prep_filled"), sem("row_copied"), sem("col_copied")
        s1_filled, s1_read, max_step, parts_done = sem("s1_filled"), sem("s1_read"), sem("max_step"), sem("parts_done")
        shift_filled, shift_done = sem("shift_filled"), sem("shift_done")
        st_filled, exp_done, pv_done, zT_copied = sem("st_filled"), sem("exp_done"), sem("pv_done"), sem("zT_copied")
        back_filled, rden_done, zn_done = sem("back_filled"), sem("rden_done"), sem("zn_done")
        slab_done, o_t, o_copied, o_mm, o_add = sem("slab_done"), sem("o_t"), sem("o_copied"), sem("o_mm"), sem("o_add")

        def run(eng, before, body, after):
            before()
            body(0, 0, True, False)
            with eng.Fori(0, N // 2 - 1) as i:
                body(2 * i + 1, 1, False, False)
                body(2 * i + 2, 0, False, False)
            body(N - 1, 1, False, True)
            after()

        with nc.Block() as block:

            @block.sync
            def _(sp):
                sp.dma_start(wout[:], keep.dram["l1_wo"]).then_inc(w_loaded, 16)
                sp.wait_ge(w_loaded, 16)

            @block.gpsimd
            def _(pool):
                def stage_quad(n, par, first=False):
                    b, g = (n >> 2) & 3, n & 3
                    if first:
                        pool.wait_ge(cleared, 6)
                    else:
                        pool.wait_ge(row_copied, 4 * n)
                        pool.wait_ge(col_copied, 2 * n)
                        pool.nop(nofuse=True)
                    for _, parts, at in PARTS:
                        for side in range(2):
                            pool.tensor_copy(stage[:, side, :, :, at[side]:at[side] + L1_HD],
                                             keep.qk3[:, bass.ds(b * TILES, TILES), parts[side], bass.ds(side * HEADS + g * QUAD, QUAD), :]).then_inc(staged, 1)
                    if not first:
                        pool.wait_ge(pv_done, 16 * (n - 1) + 2)
                        pool.nop(nofuse=True)
                    pool.tensor_copy(val[par][:, :, :, 0:L1_HD], keep.v1[:, bass.ds(b * TILES, TILES), bass.ds(g * QUAD, QUAD), :]).then_inc(val_staged, 1)

                pool.memset(stage[:], 0.0).then_inc(cleared, 1)
                for s in range(2):
                    pool.memset(val[s][:], 0.0).then_inc(cleared, 1)
                    pool.memset(rowT[s][:], 0.0).then_inc(rows_cleared, 1)
                pool.wait_ge(cleared, 3)
                pool.memset(stage[:, 1, :, :, MAX_ROW:MAX_ROW + 2], -1.0).then_inc(cleared, 1)
                for s in range(2):
                    pool.memset(val[s][:, :, :, L1_HD:L1_HD + 1], 1.0).then_inc(cleared, 1)
                stage_quad(0, 0, True)
                for b in range(BATCH):
                    rows = keep.xres[:, b * TILES:(b + 1) * TILES, :]
                    pool.tensor_tensor(rows, rows, keep.bias1[:].rearrange("p (a c) -> p a c", a=1).broadcast_to([P, TILES, P]), ALU.add).then_inc(biased, 1)
                with pool.Fori(0, N // 2 - 1) as i:
                    stage_quad(2 * i + 1, 1)
                    stage_quad(2 * i + 2, 0)
                stage_quad(N - 1, 1)
                with pool.Fori(0, BATCH // 2) as i:
                    for k in range(2):
                        b = 2 * i + k
                        pool.wait_ge(zn_done, 2 * N)
                        pool.wait_ge(o_t, 2 * b + 1)
                        pool.nop(nofuse=True)
                        pool.tensor_copy(slab[:, k], zn[:, bass.ds(b * TILES, TILES), :]).then_inc(slab_done, 1)

            @block.tensor
            def _(pe):
                def prep(n, par, k, reader):
                    reader()
                    if k == 0:
                        pe.wait_ge(staged, STAGED * (n + 1))
                    for t in range(TILES):
                        last = pe.transpose(miscb[:, t * P:(t + 1) * P],
                                            stage[:, k % 2, t, 2 * (k // 2):2 * (k // 2) + 2, :].rearrange("p h r -> p (h r)"), keep.identb[:])
                    last.then_inc(prep_filled, 1)

                def first(n, par, r):
                    h, t, half = r // 16, r % 16 // 2, r % 2
                    if r % 32 == 0:
                        pe.wait_ge(row_copied, 4 * n + 2 * (h // 2) + 2)
                        pe.wait_ge(col_copied, 2 * n + h // 2 + 1)
                    pe.wait_ge(s1_read, FIRST * n + r + 1)
                    pe.matmul(ps[:, S1 + half, :], rowT[par][:, h, t * P:(t + 1) * P],
                              colT[par][:, h // 2, half * 512:(half + 1) * 512], start=True, stop=True).then_inc(s1_filled, 1)

                def shift(n, par, pair, reader):
                    reader()
                    pe.wait_ge(parts_done, QUAD * n + 2 * pair + 2)
                    for k in range(2):
                        for t in range(TILES):
                            last = pe.transpose(miscb[64 * k + MAX_ROW:64 * k + MAX_ROW + 2, t * P:(t + 1) * P],
                                                max_parts[:, 2 * pair + k, t, :], keep.identb[:])
                    last.then_inc(shift_filled, 1)

                def second(n, par, u, k):
                    half, j, pair = u // 16, u % 16 // 2, u % 2
                    if k == 0:
                        if u < 2:
                            pe.wait_ge(shift_done, QUAD * n + 2 * pair + 2)
                        pe.wait_ge(exp_done, ST * n + u + 1)
                    last = pe.matmul(ps[:, STB + 2 * (u % 2) + k, :], colT[par][:, pair, j * P:(j + 1) * P],
                                     rowT[par][:, 2 * pair + k, half * 512:(half + 1) * 512], start=True, stop=True)
                    if k == 1:
                        last.then_inc(st_filled, 1)

                def values(n, par, r):
                    half, j = r // TILES, r % TILES
                    if r == 0:
                        pe.wait_ge(val_staged, n + 1)
                    if j == 0:
                        pe.wait_ge(zT_copied, 2 * n + half + 1)
                    pe.wait_ge(exp_done, ST * n + 2 * r + 4)
                    for h in range(QUAD):
                        last = pe.matmul(ps[VC * h:VC * (h + 1), ZB, :], val[par][:, j, h, :], prob[:, r % 2, h, :],
                                         start=(j == 0), stop=(j == TILES - 1))
                    last.then_inc(pv_done, 1)

                def back(n, half, reader):
                    reader()
                    pe.wait_ge(zT_copied, 2 * n + half + 2)
                    for t in range(4):
                        last = pe.transpose(ps[:, MISC, t * P:(t + 1) * P], zT[:, half, t * P:(t + 1) * P], keep.ident[:])
                    last.then_inc(back_filled, 1)

                def before():
                    pe.sem_inc(o_t, 3)
                    pe.wait_ge(w_loaded, 16)
                    prep(0, 0, 0, lambda: None)
                    for k in range(1, 4):
                        prep(0, 0, k, lambda: pe.wait_ge(*((row_copied, 2), (col_copied, 1), (row_copied, 4))[k - 1]))
                    for r in range(FIRST):
                        first(0, 0, r)
                    shift(0, 0, 0, lambda: pe.wait_ge(col_copied, 2))
                    shift(0, 0, 1, lambda: pe.wait_ge(shift_done, 2))

                def body(n, par, is_first, is_last):
                    nx = 1 - par
                    for s in range(ST):
                        pieces = [] if is_last else list(range(first_until[s - 1] if s else 0, first_until[s]))
                        for k in range(2):
                            second(n, par, s, k)
                            if pieces:
                                first(n + 1, nx, pieces.pop(0))
                        if s % 2 == 1:
                            if s > 1:
                                values(n, par, (s - 3) // 2)
                            elif not is_first:
                                values(n - 1, nx, 15)
                        if s == 4 and not is_first:
                            back(n - 1, 1, (lambda: pe.wait_ge(shift_done, QUAD * n + 4)) if is_last else (lambda: pe.wait_ge(col_copied, 2 * n + 4)))
                        if s == 20:
                            back(n, 0, (lambda: pe.wait_ge(zn_done, 2 * n)) if is_last else (lambda: pe.wait_ge(shift_done, QUAD * (n + 1) + 2)))
                        if is_last:
                            continue
                        if s < 4:
                            prep(n + 1, nx, s, lambda: pe.wait_ge(*((shift_done, QUAD * n + 4), (row_copied, 4 * n + 6),
                                                                     (col_copied, 2 * n + 3), (row_copied, 4 * n + 8))[s]))
                        if s == 18:
                            shift(n + 1, nx, 0, (lambda: pe.wait_ge(col_copied, 4)) if is_first else (lambda: pe.wait_ge(zn_done, 2 * n)))
                        if s == 30:
                            shift(n + 1, nx, 1, lambda: pe.wait_ge(zn_done, 2 * n + 1))
                        for r in pieces:
                            first(n + 1, nx, r)

                def after():
                    values(N - 1, 1, 15)
                    back(N - 1, 1, lambda: pe.wait_ge(zn_done, 2 * N - 1))
                    pe.wait_ge(zn_done, 2 * N)

                run(pe, before, body, after)
                with pe.Fori(0, BATCH // 2) as i:
                    for k in range(2):
                        b = 2 * i + k
                        pe.wait_ge(slab_done, b + 1)
                        for half in range(2):
                            u = 2 * b + half
                            pe.wait_ge(o_copied, u + 1)
                            for t in range(4):
                                last = pe.transpose(ps[:, S1 + half, t * P:(t + 1) * P], slab[:, k, 4 * half + t, :], keep.ident[:])
                            last.then_inc(o_t, 1)
                            pe.wait_ge(o_copied, u + 3)
                            pe.wait_ge(o_add, u + 1)
                            for t in range(4):
                                last = pe.matmul(ps[:, STB + half, t * P:(t + 1) * P], znT[:, half, t * P:(t + 1) * P], wout[:], start=True, stop=True)
                            last.then_inc(o_mm, 1)

            @block.vector
            def _(dve):
                def reduce(n, r):
                    h, t, half = r // 16, r % 16 // 2, r % 2
                    dve.wait_ge(s1_filled, FIRST * n + r + 1)
                    dve.tensor_reduce(row_max[:, h, t, half:half + 1], ps[:, S1 + half, :], AX.X, ALU.max).then_inc(s1_read, 1)
                    if r >= 16 and r % 16 < 3:
                        split_max(n, h - 1, r % 16)
                    if r == FIRST - 1:
                        for k in range(3):
                            split_max(n, h, k)

                def split_max(n, h, k):
                    if k == 0:
                        dve.wait_ge(s1_read, FIRST * n + 16 * (h + 1) + 2)
                        dve.tensor_tensor(max_of[:, h, :], row_max[:, h, :, 0], row_max[:, h, :, 1], ALU.max).then_inc(max_step, 1)
                    elif k == 1:
                        dve.wait_ge(max_step, 2 * (QUAD * n + h) + 1)
                        dve.tensor_copy(max_parts[:, h, :, 0], max_of[:, h, :]).then_inc(max_step, 1)
                    else:
                        dve.wait_ge(max_step, 2 * (QUAD * n + h) + 2)
                        dve.tensor_tensor(max_parts[:, h, :, 1], max_of[:, h, :], max_parts[:, h, :, 0], ALU.subtract).then_inc(parts_done, 1)

                def copy_rows(n, par, pair):
                    dve.wait_ge(prep_filled, 4 * n + 2 * pair + 1)
                    for k in range(2):
                        o = slice(ROWS * k, ROWS * (k + 1))
                        dve.tensor_copy(rowT[par][o, 2 * pair + k, :], miscb[o]).then_inc(row_copied, 1)

                def normalize(n, half):
                    z = ps[:, MISC, :].rearrange("p (t h c) -> p t h c", t=4, h=QUAD)
                    dve.wait_ge(back_filled, 2 * n + half + 1)
                    dve.reciprocal(rden[:].rearrange("p t (h x) -> p t h x", x=1), z[:, :, :, L1_HD:L1_HD + 1]).then_inc(rden_done, 1)
                    dve.wait_ge(rden_done, 2 * n + half + 1)
                    dst = zn[:, bass.ds(((n >> 2) & 3) * TILES + 4 * half, 4), bass.ds((n & 3) * QUAD * L1_HD, QUAD * L1_HD)]
                    dve.tensor_tensor(dst.rearrange("p t (h d) -> p t h d", h=QUAD), z[:, :, :, 0:L1_HD],
                                      rden[:].rearrange("p t (h x) -> p t h x", x=1).broadcast_to([P, 4, QUAD, L1_HD]), ALU.mult).then_inc(zn_done, 1)

                def before():
                    dve.sem_inc(s1_read, 2)
                    dve.wait_ge(rows_cleared, 2)
                    for pair in range(2):
                        copy_rows(0, 0, pair)
                    for r in range(FIRST):
                        reduce(0, r)

                def body(n, par, is_first, is_last):
                    for s in range(ST):
                        if s == 4 and not is_first:
                            normalize(n - 1, 1)
                        if s == 20:
                            normalize(n, 0)
                        if is_last:
                            continue
                        if s in (0, 2):
                            copy_rows(n + 1, 1 - par, s // 2)
                        for r in range(first_until[s - 1] if s else 0, first_until[s]):
                            reduce(n + 1, r)

                run(dve, before, body, lambda: normalize(N - 1, 1))
                dve.wait_ge(biased, BATCH)
                dve.sem_inc(o_add, 2)
                with dve.Fori(0, BATCH // 2) as i:
                    for k in range(2):
                        for half in range(2):
                            u = 4 * i + 2 * k + half
                            rows = keep.xres[:, bass.ds(4 * u, 4), :]
                            dve.wait_ge(o_mm, u + 1)
                            dve.tensor_tensor(rows, ps[:, STB + half, :].rearrange("p (t c) -> p t c", t=4), rows, ALU.add).then_inc(o_add, 1)

            @block.scalar
            def _(act):
                def exponentials(n, u):
                    r, pair = u // 2, u % 2
                    act.wait_ge(st_filled, ST * n + u + 1)
                    if pair == 0:
                        act.wait_ge(pv_done, 16 * n + r + 1)
                    act.activation(prob[:, r % 2, 2 * pair:2 * pair + 2, :], ps[:, STB + 2 * pair:STB + 2 * pair + 2, :], ACT.Exp,
                                   scale=scale).then_inc(exp_done, 1)

                def copy_cols(n, par, pair):
                    act.wait_ge(prep_filled, 4 * n + 2 * pair + 2)
                    act.copy(colT[par][:, pair, :], miscb).then_inc(col_copied, 1)

                def copy_shift(n, par, pair):
                    act.wait_ge(shift_filled, 2 * n + pair + 1)
                    for k in range(2):
                        o = slice(64 * k + MAX_ROW, 64 * k + MAX_ROW + 2)
                        act.copy(rowT[par][o, 2 * pair + k, :], miscb[o]).then_inc(shift_done, 1)

                def copy_zT(n, half):
                    act.wait_ge(pv_done, 16 * n + 8 * half + 10)
                    act.copy(zT[:, half, :], ps[:, ZB, :]).then_inc(zT_copied, 1)

                def before():
                    act.sem_inc(exp_done, 2)
                    act.sem_inc(pv_done, 2)
                    act.sem_inc(zT_copied, 1)
                    act.sem_inc(o_copied, 2)
                    for pair in range(2):
                        copy_cols(0, 0, pair)
                    for pair in range(2):
                        copy_shift(0, 0, pair)

                def body(n, par, is_first, is_last):
                    for s in range(ST):
                        exponentials(n, s)
                        if s == 2 and not is_first:
                            copy_zT(n - 1, 1)
                        if s == 18:
                            copy_zT(n, 0)
                        if is_last:
                            continue
                        if s in (1, 3):
                            copy_cols(n + 1, 1 - par, s // 2)
                        if s in (18, 30):
                            copy_shift(n + 1, 1 - par, (s - 18) // 12)

                run(act, before, body, lambda: copy_zT(N - 1, 1))
                with act.Fori(0, BATCH // 2) as i:
                    for k in range(2):
                        for half in range(2):
                            u = 4 * i + 2 * k + half
                            act.wait_ge(o_t, u + 4)
                            act.copy(znT[:, half, :], ps[:, S1 + half, :]).then_inc(o_copied, 1)


def build(nc, dram, out):
    with ExitStack() as ctx:
        m = Mem(nc, ctx)
        keep = Keep()
        keep.dram = dram
        keep.ident = m.sb("ident", [P, P])
        keep.identb = m.sb("identb", [P, P], BF16)
        keep.neg_half = m.sb("neg_half", [P, 2 * HEADS])
        keep.y_in = m.sb("y_in", [P, BATCH * (TILES + 1) + 1, P])
        keep.y_mid = m.sb("y_mid", [P, BATCH * (TILES + 1) + 1, P])
        with ExitStack() as cx:
            mx = Mem(nc, cx)
            keep.xres = mx.sb("xres", [P, ALL_TILES, P])
            keep.bias0 = mx.sb("bias0", [P, P])
            keep.bias1 = mx.sb("bias1", [P, P])
            keep.w8 = mx.sb("w8", [P, P], BF16)
            load_phase(nc, keep, dram)
            with ExitStack() as c0:
                keep.xnT = Mem(nc, c0).sb("xnT", [P, BATCH * SEQ])
                norm0_phase(nc, keep)
                causal_attention_phase(nc, keep)
            with ExitStack() as c1:
                keep.qk3 = Mem(nc, c1).sb("qk3", [P, ALL_TILES, SPLIT, 2 * HEADS, L1_HD], BF16)
                keep.v1 = Mem(nc, c1).sb("v1", [P, ALL_TILES, HEADS, L1_HD])
                norm1_phase(nc, keep)
                full_attention_phase(nc, keep)
            parked = nc.dram_tensor("parked_x", [P, ALL_TILES, P], F32).ap()
            parked_done = mx.sem("parked_done")
            with nc.Block() as block:

                @block.sync
                def _(sp):
                    sp.dma_start(parked, keep.xres[:]).then_inc(parked_done, 16)
                    sp.wait_ge(parked_done, 16)
        local_phase(nc, keep)
        output_phase(nc, keep, parked, out)


LOCAL_ORDER = [("QK0", 0), ("T3", -1), (9, 0), (10, 0), ("E0", 0), ("PV3", -1), (1, 1), ("QK1", 0), ("TZ1", -1),
               (2, 1), ("T0", 0), ("WO", -1), (3, 1), ("E1", 0), (4, 1), ("PV0", 0), ("QK2", 0), ("T1", 0), (5, 1),
               ("E2", 0), (6, 1), ("PV1", 0), ("QK3", 0), ("T2", 0), (7, 1), (8, 1), ("TZ0", 0), ("E3", 0),
               ("PV2", 0), (0, 2)]
POOL_ORDER = [(10, 0), (0, 2), (8, 1), (1, 1), (2, 1), (3, 1), (4, 1)]

VECTOR_ORDER = [x for x in LOCAL_ORDER if x != ("PV0", 0)]
VECTOR_ORDER.insert(VECTOR_ORDER.index((4, 1)), ("PV0", 0))


def operand_use(k, n, tile):
    known = isinstance(tile, int)
    if k == 0:
        return 6 * n - (0 if known and tile == 0 else 1)
    if k == 10:
        return 6 * n + (5 if known and tile == ALL_TILES - 1 else 6)
    return 6 * n + k // 2 if k % 2 == 0 else 5 * n + k // 2


T_INDEX = {"T0": 0, "T1": 1, "T2": 2, "TZ0": 3, "T3": 4, "TZ1": 5}
Z_INDEX = {"PV0": 0, "PV1": 1, "PV2": 2, "PV3": 3, "WO": 4}
FF_LAG = 4
HALF = DIM // 2


def local_phase(nc, keep):
    UC = [(0, P), (P, P), (2 * P, DIM_INNER - 2 * P)]
    with ExitStack() as ctx:
        m = Mem(nc, ctx)
        wqkv = m.sb("lo_wqkv", [P, 2, 3 * INNER])
        wo = m.sb("lo_wo", [P, 2, INNER])
        w1 = m.sb("lo_w1", [P, 2, 2 * DIM_INNER])
        w2 = m.sb("lo_w2", [P, 2, 3 * P])
        b1 = m.sb("lo_b1", [P, 2, 2 * DIM_INNER])
        b2 = m.sb("lo_b2", [P, 2, DIM])
        ln = m.sb("lo_ln", [P, DEPTH, 2])
        scales = m.sb("lo_scales", [P, DEPTH + 1, 4, LOC_HD])
        rotary = m.sb("lo_rotary", [P, 4, TILES, LOC_HD])
        tables = m.sb("lo_tables", [P, 4, TILES, LOC_HD])
        mask = m.sb("lo_mask", [P, TILES, LOC_KEYS], BF16)
        has_prev = m.sb("lo_has_prev", [P, TILES])
        shift = m.sb("lo_shift", [P, 2, P])
        rows = [m.sb(f"lo_rows{s}", [P, P]) for s in range(2)]
        prev = [m.sb(f"lo_prev{s}", [P, HALF]) for s in range(2)]
        xT = [m.sb(f"lo_xT{s}", [P, P]) for s in range(2)]
        qT = [m.sb(f"lo_qT{s}", [P, HEADS, P]) for s in range(2)]
        kT = [m.sb(f"lo_kT{s}", [P, PAIRS, LOC_KEYS]) for s in range(2)]
        val = [m.sb(f"lo_val{s}", [P, HEADS, VW]) for s in range(2)]
        tail = [m.sb(f"lo_tail{s}", [P, GROUPS, GROUP, VW]) for s in range(2)]
        square = m.sb("lo_square", [P, 2, 512])
        by_cos = m.sb("lo_by_cos", [P, 2, 512])
        by_sin = m.sb("lo_by_sin", [P, 2, 512])
        rot = m.sb("lo_rot", [P, 4, 8, LOC_HD])
        unit = m.sb("lo_unit", [P, 4, 8, LOC_HD])
        sumsq = m.sb("lo_sumsq", [P, 4, 8])
        norm = m.sb("lo_norm", [P, 4, 8])
        rnorm = m.sb("lo_rnorm", [P, 4, 8])
        row_max = m.sb("lo_row_max", [P, 2, GROUP])
        diff = m.sb("lo_diff", [P, 2, GROUP, LOC_KEYS])
        prob = m.sb("lo_prob", [P, 2, GROUP, P])
        prob_prev = m.sb("lo_prob_prev", [WINDOW, 2, GROUP, WINDOW])
        probT = m.sb("lo_probT", [P, 2, GROUP, P])
        tailT = m.sb("lo_tailT", [P, 2, WINDOW])
        rden = m.sb("lo_rden", [P, GROUP])
        zn = m.sb("lo_zn", [P, HEADS, LOC_HD])
        znT = m.sb("lo_znT", [P, PAIRS, P])
        stats = m.sb("ff_stats", [P, 6])
        meanvar = m.sb("ff_meanvar", [P, 2, 2])
        var = m.sb("ff_var", [P, 1])
        rstd = m.sb("ff_rstd", [P, 1])
        a_sb, gate, gelu = (b[:, :, 0:DIM_INNER] for b in (square, by_cos, by_sin))
        prod = rot[:].rearrange("p (s c) h d -> p s (c h d)", s=2)[:, :, 0:DIM_INNER]
        prodT = probT[:, :, 0:3, :]
        xs, xn, xnT, yb = (znT[:, 2 * k:2 * k + 2, :] for k in range(4))
        ps = m.ps("lo_ps", [P, 8, 512])
        S_BANK, T_BANK, Z_BANK, F_BANK = 0, 4, 5, 6
        A_BANK, B_BANK, H_BANK, D_BANK, E_BANK = 0, 1, 2, 6, 7

        sem = {}

        def S(name):
            if name not in sem:
                sem[name] = m.sem("lo_" + name)
            return sem[name]

        loaded, consts, tables_done = S("loaded"), S("consts"), S("tables_done")
        w_loaded = S("w_loaded")
        rows_staged, xT_done = S("rows_staged"), S("xT_done")
        f_filled, f_free = [S(f"f_filled{k}") for k in range(2)], [S(f"f_free{k}") for k in range(2)]
        squared, rot_parts, sumsq_done, rot_done = S("squared"), S("rot_parts"), S("sumsq_done"), S("rot_done")
        clamped, rnorm_done, unit_done = S("clamped"), S("rnorm_done"), S("unit_done")
        tail_done = [S(f"tail_done{k}") for k in range(2)]
        val_done, qkT_done, kprev_done = S("val_done"), S("qkT_done"), S("kprev_done")
        prev_exp_done = S("prev_exp_done")
        scored, max_done, diff_done, exp_done = S("scored"), S("max_done"), S("diff_done"), S("exp_done")
        t_filled, t_free, tailT_done = S("t_filled"), S("t_free"), S("tailT_done")
        z_filled, z_free, rden_done, zn_done, znT_done = S("z_filled"), S("z_free"), S("rden_done"), S("zn_done"), S("znT_done")
        mid_done, out_done = S("mid_done"), S("out_done")
        a_filled, xs_half, xs_done, stats_done, mv_done = S("a_filled"), S("xs_half"), S("xs_done"), S("stats_done"), S("mv_done")
        var_done, rstd_done, xn_done, b_filled, xnT_done = S("var_done"), S("rstd_done"), S("xn_done"), S("b_filled"), S("xnT_done")
        h_filled, a_done, gate_done, gelu_done, prod_done = S("h_filled"), S("a_done"), S("gate_done"), S("gelu_done"), S("prod_done")
        d_filled, prodT_done, e_filled, yb_done = S("d_filled"), S("prodT_done"), S("e_filled"), S("yb_done")
        W_DMAS = 7

        def slot_of(tile):
            return tile + (tile >> 3) + 1

        def at(buf, tile, back=0):
            return buf[:, bass.ds(slot_of(tile) - back, 1), :].rearrange("p a c -> p (a c)")

        def attention_steps(eng, l, front, back, order=LOCAL_ORDER):
            def cycle(c, par):
                for piece, off in order:
                    if isinstance(c, int) and not 0 <= c + off < ALL_TILES:
                        continue
                    (front if isinstance(piece, int) else back)(l, c + off, (par + off) % 2, piece)
            for c in (-2, -1, 0):
                cycle(c, c % 2)
            with eng.Fori(0, (ALL_TILES - 4) // 4) as i:
                for k in range(1, 5):
                    cycle(4 * i + k, k % 2)
            for c in range(ALL_TILES - 3, ALL_TILES + 1):
                cycle(c, c % 2)

        def ff_steps(eng, l, step):
            def one(s, par):
                known = isinstance(s, int)
                step(l,
                     s if not known or s < ALL_TILES else None,
                     s - 2 if not known or 0 <= s - 2 < ALL_TILES else None,
                     s - FF_LAG if not known or s - FF_LAG >= 0 else None, par)
            for s in range(4):
                one(s, s % 2)
            with eng.Fori(1, ALL_TILES // 4) as i:
                for k in range(4):
                    one(4 * i + k, k % 2)
            for s in range(ALL_TILES, ALL_TILES + FF_LAG):
                one(s, s % 2)

        with nc.Block() as block:

            @block.sync
            def _(sp):
                for dst, src in ((ln, "ln"), (rotary, "lo_rotary"), (mask, "lo_mask"), (shift, "lo_shift")):
                    sp.dma_start(dst[:], keep.dram[src]).then_inc(loaded, 16)
                sp.dma_start(scales[:, 0:DEPTH], keep.dram["lo_scales"].rearrange("(a l) k d -> a l k d", a=1).broadcast_to([P, DEPTH, 4, LOC_HD])).then_inc(loaded, 16)

                def load_layer(l, slot):
                    one = bass.ds(l, 1)
                    for dst, name in ((wqkv, "Wqkv"), (w1, "W1")):
                        sp.dma_start(dst[:, slot, :], keep.dram[name][one].rearrange("a p n -> p (a n)")).then_inc(w_loaded, 16)
                    sp.dma_start(wo[:, slot, :].rearrange("p (k e) -> p k e", e=DIM),
                                 keep.dram["Wo"][one].rearrange("a (k p) e -> p (a k) e", p=P)).then_inc(w_loaded, 16)
                    sp.dma_start(w2[:, slot, 0:2 * P].rearrange("p (k e) -> p k e", e=DIM),
                                 keep.dram["W2"][one, 0:2 * P].rearrange("a (k p) e -> p (a k) e", p=P)).then_inc(w_loaded, 16)
                    sp.dma_start(w2[0:UC[2][1], slot, 2 * P:], keep.dram["W2"][one, 2 * P:].rearrange("a p e -> p (a e)")).then_inc(w_loaded, 16)
                    sp.dma_start(b1[:, slot, :], keep.dram["b1"][one].broadcast_to([P, 2 * DIM_INNER])).then_inc(w_loaded, 16)
                    sp.dma_start(b2[:, slot, :], keep.dram["b2"][one].broadcast_to([P, DIM])).then_inc(w_loaded, 16)

                def tails(l, tile, par):
                    n = l * ALL_TILES + tile
                    sp.wait_ge(val_done, 2 * n + 2)
                    sp.wait_ge(zn_done, 4 * n + 4)
                    v = val[1 - par][P - WINDOW:P].rearrange("p (g j) d -> p g j d", j=GROUP)
                    for j in range(GROUP):
                        sp.dma_start(tail[par][j * WINDOW:(j + 1) * WINDOW, :, j, :], v[:, :, j, :]).then_inc(tail_done[par], 16)

                load_layer(0, 0)
                sp.wait_ge(consts, 1)

                def layer(l, par, more):
                    with sp.Fori(0, ALL_TILES // 2) as i:
                        tails(l, 2 * i, 0)
                        tails(l, 2 * i + 1, 1)
                    if more:
                        sp.wait_ge(mid_done, l * ALL_TILES + 1)
                        load_layer(l + 1, 1 - par)
                    sp.wait_ge(out_done, (l + 1) * ALL_TILES + 2)
                    sp.nop(nofuse=True)
                with sp.Fori(0, DEPTH // 2 - 1) as h:
                    layer(2 * h, 0, True)
                    layer(2 * h + 1, 1, True)
                layer(DEPTH - 2, 0, True)
                layer(DEPTH - 1, 1, False)
                for k in range(2):
                    sp.wait_ge(tail_done[k], 16 * GROUP * DEPTH * ALL_TILES // 2)
                sp.wait_ge(w_loaded, 16 * W_DMAS * DEPTH)

            @block.gpsimd
            def _(pool):
                for s in range(2):
                    pool.memset(tail[s][:], 0.0).then_inc(S("pool_init"), 1)
                    pool.memset(val[s][:], 1.0).then_inc(S("pool_init"), 1)
                    pool.memset(kT[s][:], 0.0).then_inc(S("pool_init"), 1)
                    pool.memset(qT[s][:], 0.0).then_inc(S("pool_init"), 1)
                pool.memset(scales[:, DEPTH], 0.0).then_inc(S("pool_init"), 1)
                pool.memset(has_prev[:, 0:1], 0.0).then_inc(S("pool_init"), 1)
                pool.memset(has_prev[:, 1:TILES], 1.0).then_inc(S("pool_init"), 1)
                pool.wait_ge(S("pool_init"), 11)
                pool.sem_inc(consts, 1)
                pool.sem_inc(unit_done, 1)
                pool.wait_ge(loaded, 80)

                def make_tables(l):
                    for k in range(4):
                        pool.tensor_tensor(tables[:, k], rotary[:, k],
                                           scales[:, bass.ds(l, 1), k].rearrange("p a d -> p a d").broadcast_to([P, TILES, LOC_HD]),
                                           ALU.mult).then_inc(tables_done, 1)

                def front(l, tile, par, k):
                    n = l * ALL_TILES + tile
                    if k == 0:
                        pool.wait_ge(xT_done, n + 1)
                        pool.nop(nofuse=True)
                        pool.tensor_copy(rows[par][:], at(keep.y_in, tile)).then_inc(rows_staged, 1)
                        pool.tensor_copy(prev[par][:], at(keep.y_in, tile, 1)[:, HALF:]).then_inc(rows_staged, 1)
                    if 1 <= k <= 4:
                        pool.wait_ge(rot_parts, 3 * (4 * n + k))
                        pool.tensor_tensor(rot[:, k - 1].rearrange("p h d -> p (h d)"), by_cos[:, k % 2], by_sin[:, k % 2], ALU.add).then_inc(rot_done, 1)
                    if k in (2, 4):
                        a, b = k - 2, k
                        pool.wait_ge(sumsq_done, 4 * n + k + 2)
                        pool.nop(nofuse=True)
                        pool.tensor_scalar(norm[:, a:b], sumsq[:, a:b], 1e-24, None, ALU.max).then_inc(clamped, 1)
                        pool.wait_ge(clamped, 2 * n + k // 2)
                        pool.tensor_tensor(rnorm[:, a:b].rearrange("p c h -> p (c h)"), norm[:, a:b].rearrange("p c h -> p (c h)"),
                                           keep.neg_half[:, 0:2 * 8], ALU.pow).then_inc(rnorm_done, 1)
                        pool.wait_ge(rnorm_done, 2 * n + k // 2)
                        pool.wait_ge(rot_done, 4 * n + k + 2)
                        pool.wait_ge(f_free[0], 6 * n + (1 if isinstance(tile, int) and tile == 0 else 2))
                        pool.wait_ge(f_free[1], 5 * n + 1)
                        pool.tensor_tensor(unit[:, a:b].rearrange("p c h d -> p (c h) d"), rot[:, a:b].rearrange("p c h d -> p (c h) d"),
                                           rnorm[:, a:b].rearrange("p c (h x) -> p (c h) x", x=1).broadcast_to([P, 16, LOC_HD]),
                                           ALU.mult).then_inc(unit_done, 1)
                    if k in (8, 10):
                        h = slice(0, 4) if k == 8 else slice(4, 8)
                        pool.wait_ge(qkT_done, 6 * n + (3 if k == 8 else 6))
                        pool.wait_ge(diff_done, 4 * n + 4)
                        pool.nop(nofuse=True)
                        pool.tensor_tensor(kT[par][:, h, 0:WINDOW], kT[1 - par][:, h, P:LOC_KEYS],
                                           has_prev[:, bass.ds(tile & (TILES - 1), 1)].rearrange("p (a b) -> p a b", b=1).broadcast_to([P, 4, WINDOW]),
                                           ALU.mult).then_inc(kprev_done, 1)

                def ff(l, sa, sc, sd, par):
                    if sd is not None:
                        n = l * ALL_TILES + sd
                        pool.wait_ge(out_done, n + 1)
                        pool.nop(nofuse=True)
                        pool.tensor_tensor(yb[:, par], at(keep.y_mid, sd), b2[:, bass.ds(l & 1, 1)].rearrange("p a c -> p (a c)"), ALU.add).then_inc(yb_done, 1)
                    if sa is not None:
                        n = l * ALL_TILES + sa
                        pool.wait_ge(mv_done, n + 1)
                        pool.nop(nofuse=True)
                        pool.tensor_scalar(var[:], meanvar[:, par, 1:2], LN_EPS, None, ALU.add).then_inc(var_done, 1)
                        pool.wait_ge(var_done, n + 1)
                        pool.tensor_tensor(rstd[:], var[:], keep.neg_half[:, 0:1], ALU.pow).then_inc(rstd_done, 1)
                    if sc is not None:
                        n = l * ALL_TILES + sc
                        pool.wait_ge(a_done, n + 3)
                        pool.wait_ge(gelu_done, n + 1)
                        pool.wait_ge(prodT_done, n + 1)
                        pool.tensor_tensor(prod[:, par], a_sb[:, par], gelu[:, par], ALU.mult).then_inc(prod_done, 1)

                pool.sem_inc(prodT_done, 2)
                pool.sem_inc(xn_done, 2)
                pool.sem_inc(yb_done, 1)
                pool.sem_inc(prod_done, 2)
                pool.sem_inc(rot_done, 2)
                make_tables(0)
                with pool.Fori(0, DEPTH) as l:
                    pool.wait_ge(w_loaded, (l + 1) * 16 * W_DMAS)
                    attention_steps(pool, l, front, None, POOL_ORDER)
                    pool.wait_ge(mid_done, (l + 1) * ALL_TILES)
                    make_tables(l + 1)
                    ff_steps(pool, l, ff)
                    pool.wait_ge(out_done, (l + 1) * ALL_TILES + 2)

            @block.tensor
            def _(pe):
                def front(l, tile, par, k):
                    n = l * ALL_TILES + tile
                    bank = ps[:, F_BANK + k % 2, :]
                    pe.wait_ge(f_free[k % 2], operand_use(k, n, tile) + 1)
                    if k == 0:
                        pe.wait_ge(rows_staged, 2 * n + 2)
                        pe.matmul(bank[0:HALF, 0:P], rows[par][:, 0:HALF], keep.ident[:], start=True, stop=True)
                        pe.matmul(bank[HALF:P, 0:P], rows[par][:, HALF:], shift[:, 0, :], start=True, stop=False)
                        last = pe.matmul(bank[HALF:P, 0:P], prev[par][:], shift[:, 1, :], start=False, stop=True)
                    elif k <= 6:
                        if k == 1:
                            pe.wait_ge(xT_done, n + 3)
                        col = (k - 1) * 512 if k > 4 else (k - 1) % 2 * INNER + (k - 1) // 2 * 512
                        last = pe.matmul(bank[:], xT[par][:], wqkv[:, bass.ds(l & 1, 1), col:col + 512].rearrange("p a n -> p (a n)"),
                                         start=True, stop=True)
                    else:
                        pe.wait_ge(unit_done, 2 * n + (k - 7) // 2 + 2)
                        c = unit[:, k - 7].rearrange("p h d -> p (h d)")
                        for j in range(4):
                            last = pe.transpose(bank[:, j * P:(j + 1) * P], c[:, j * P:(j + 1) * P], keep.ident[:])
                    last.then_inc(f_filled[k % 2], 1)

                def back(l, tile, par, piece):
                    n = l * ALL_TILES + tile
                    kind, g = piece.rstrip("0123"), int(piece[-1]) if piece[-1].isdigit() else 0
                    u = 4 * n + g
                    sl = g % 2
                    scores = ps[:, S_BANK + 2 * sl:S_BANK + 2 * sl + 2, :]
                    if kind == "QK":
                        if g == 0:
                            pe.wait_ge(qkT_done, 6 * n + 9)
                            pe.wait_ge(kprev_done, 2 * n + 1)
                        if g == 2:
                            pe.wait_ge(qkT_done, 6 * n + 12)
                            pe.wait_ge(kprev_done, 2 * n + 2)
                        pe.wait_ge(tailT_done, u + 1)
                        for j in range(GROUP):
                            h = 4 * g + j
                            o = scores[:, j % 2, (j // 2) * LOC_KEYS:(j // 2 + 1) * LOC_KEYS]
                            pe.matmul(o, qT[par][:, h, :], kT[par][:, h // 2, :], start=True, stop=False)
                            last = pe.matmul(o, keep.identb[:], mask[:, bass.ds(tile & (TILES - 1), 1), :].rearrange("p a k -> p (a k)"),
                                             start=False, stop=True)
                        last.then_inc(scored, 1)
                    elif kind == "T":
                        pe.wait_ge(exp_done, u + 3)
                        pe.wait_ge(t_free, 6 * n + T_INDEX[piece] + 1)
                        for j in range(GROUP):
                            pe.transpose(ps[:, T_BANK, j * P:(j + 1) * P], prob[:, sl, j, :], keep.ident[:])
                        last = pe.transpose(scores[:, 0, 2 * LOC_KEYS:2 * LOC_KEYS + WINDOW], prob_prev[:, sl].rearrange("p j k -> p (j k)"), keep.ident[0:WINDOW, 0:WINDOW])
                        last.then_inc(t_filled, 1)
                    elif kind == "PV":
                        pe.wait_ge(t_free, 6 * n + T_INDEX[f"T{g}"] + 2)
                        pe.wait_ge(tailT_done, u + 3)
                        pe.wait_ge(z_free, 5 * n + g + 1)
                        if g == 0:
                            pe.wait_ge(val_done, 2 * n + 4)
                            pe.wait_ge(tail_done[par], 16 * GROUP * (n >> 1) + 16 * GROUP)
                        for j in range(GROUP):
                            pe.matmul(ps[:, Z_BANK, j * VW:(j + 1) * VW], probT[:, sl, j, :], val[par][:, 4 * g + j, :],
                                      start=(j == 0), stop=False, skip_group_check=True)
                        last = pe.matmul(ps[0:WINDOW, Z_BANK, 0:GROUP * VW], tailT[:, sl, :], tail[par][:, g].rearrange("p j d -> p (j d)"),
                                         start=False, stop=True, skip_group_check=True)
                        last.then_inc(z_filled, 1)
                    elif kind == "TZ":
                        pe.wait_ge(zn_done, 4 * n + 8 + 2 * g + 2)
                        pe.wait_ge(t_free, 6 * n + T_INDEX[piece] + 1)
                        flat = zn[:].rearrange("p h d -> p (h d)")
                        for j in range(4):
                            last = pe.transpose(ps[:, T_BANK, j * P:(j + 1) * P], flat[:, (4 * g + j) * P:(4 * g + j + 1) * P], keep.ident[:])
                        last.then_inc(t_filled, 1)
                    elif kind == "WO":
                        pe.wait_ge(znT_done, 2 * n + 2)
                        pe.wait_ge(z_free, 5 * n + Z_INDEX["WO"] + 1)
                        for c in range(PAIRS):
                            last = pe.matmul(ps[:, Z_BANK, 0:P], znT[:, c, :], wo[:, bass.ds(l & 1, 1), c * P:(c + 1) * P].rearrange("p a n -> p (a n)"),
                                             start=(c == 0), stop=(c == PAIRS - 1))
                        last.then_inc(z_filled, 1)

                def ff(l, sa, sc, sd, par):
                    if sc is not None:
                        n = l * ALL_TILES + sc
                        pe.wait_ge(xn_done, n + 3)
                        pe.transpose(ps[:, B_BANK, 0:P], xn[:, par], keep.ident[:]).then_inc(b_filled, 1)
                    if sa is not None:
                        n = l * ALL_TILES + sa
                        pe.wait_ge(xs_done, n + 1)
                        pe.matmul(ps[:, A_BANK, 0:HALF], shift[:, 0, :], at(keep.y_mid, sa)[:, HALF:], start=True, stop=False)
                        pe.matmul(ps[:, A_BANK, 0:HALF], shift[:, 1, :], at(keep.y_mid, sa, 1)[:, HALF:], start=False, stop=True).then_inc(a_filled, 1)
                    if sd is not None:
                        n = l * ALL_TILES + sd
                        pe.wait_ge(prod_done, n + 3)
                        for c, (o, w) in enumerate(UC):
                            last = pe.transpose(ps[0:w, D_BANK, c * P:(c + 1) * P], prod[:, par, o:o + w], keep.ident[:])
                        last.then_inc(d_filled, 1)
                    if sc is not None:
                        n = l * ALL_TILES + sc
                        pe.wait_ge(xnT_done, n + 1)
                        pe.wait_ge(a_done, n + 1)
                        for k in range(2):
                            last = pe.matmul(ps[:, H_BANK + 2 * par + k, 0:DIM_INNER], xnT[:, par],
                                             w1[:, bass.ds(l & 1, 1), k * DIM_INNER:(k + 1) * DIM_INNER].rearrange("p a n -> p (a n)"), start=True, stop=True)
                        last.then_inc(h_filled, 1)
                    if sd is not None:
                        n = l * ALL_TILES + sd
                        pe.wait_ge(prodT_done, n + 3)
                        pe.wait_ge(out_done, n + 2)
                        for c, (o, w) in enumerate(UC):
                            last = pe.matmul(ps[:, E_BANK, 0:P], prodT[0:w, par, c, :], w2[0:w, bass.ds(l & 1, 1), c * P:(c + 1) * P].rearrange("p a n -> p (a n)"),
                                             start=(c == 0), stop=(c == 2))
                        last.then_inc(e_filled, 1)

                pe.wait_ge(loaded, 80)
                with pe.Fori(0, DEPTH) as l:
                    pe.wait_ge(w_loaded, (l + 1) * 16 * W_DMAS)
                    attention_steps(pe, l, front, back)
                    pe.wait_ge(mid_done, (l + 1) * ALL_TILES)
                    ff_steps(pe, l, ff)
                    pe.wait_ge(out_done, (l + 1) * ALL_TILES + 2)

            @block.vector
            def _(dve):
                dve.wait_ge(loaded, 80)
                dve.sem_inc(f_free[0], 1)
                dve.sem_inc(f_free[1], 1)
                dve.sem_inc(diff_done, 8)
                dve.sem_inc(z_free, 1)
                dve.sem_inc(zn_done, 8)
                dve.sem_inc(xs_done, 1)
                dve.sem_inc(a_done, 2)
                dve.sem_inc(sumsq_done, 2)
                dve.sem_inc(out_done, 2)
                dve.wait_ge(tables_done, 4)

                def front(l, tile, par, k):
                    if not 1 <= k <= 4:
                        return
                    n = l * ALL_TILES + tile
                    c = 4 * n + k - 1
                    t = tile & (TILES - 1)
                    rows_q = ps[:, F_BANK + k % 2, :].rearrange("p (h d) -> p h d", d=LOC_HD)
                    side = 2 * ((k - 1) % 2)
                    h = LOC_HD // 2

                    def table(which, lo, hi):
                        tab = tables[:].rearrange("p k t d -> p (k t) d")[:, bass.ds((side + which) * TILES + t, 1), lo:hi]
                        return tab.broadcast_to([P, 8, hi - lo])

                    if k == 1:
                        dve.wait_ge(tables_done, 4 * l + 4)
                    dve.wait_ge(squared, c + 1)
                    dve.wait_ge(rot_done, c + 1)
                    oc = by_cos[:, k % 2].rearrange("p (h d) -> p h d", d=LOC_HD)
                    os_ = by_sin[:, k % 2].rearrange("p (h d) -> p h d", d=LOC_HD)
                    dve.tensor_tensor(oc, rows_q, table(0, 0, LOC_HD), ALU.mult).then_inc(rot_parts, 1)
                    dve.tensor_tensor(os_[:, :, 0:h], rows_q[:, :, h:], table(1, 0, h), ALU.mult).then_inc(rot_parts, 1)
                    dve.tensor_tensor(os_[:, :, h:], rows_q[:, :, 0:h], table(1, h, LOC_HD), ALU.mult).then_inc(rot_parts, 1)
                    dve.tensor_reduce(sumsq[:, k - 1, :], square[:, k % 2].rearrange("p (h d) -> p h d", d=LOC_HD), AX.X, ALU.add).then_inc(sumsq_done, 1)
                    dve.wait_ge(rot_parts, 3 * (c + 1))
                    dve.sem_inc(f_free[k % 2], 1)

                def back(l, tile, par, piece):
                    n = l * ALL_TILES + tile
                    kind, g = piece.rstrip("0123"), int(piece[-1]) if piece[-1].isdigit() else 0
                    u = 4 * n + g
                    sl = g % 2
                    if kind == "QK":
                        s4 = ps[:, S_BANK + 2 * sl:S_BANK + 2 * sl + 2, 0:2 * LOC_KEYS].rearrange("p b (j k) -> p b j k", k=LOC_KEYS)
                        dve.wait_ge(scored, u + 1)
                        dve.tensor_reduce(row_max[:, sl, :].rearrange("p (b j) -> p b j", b=2), s4, AX.X, ALU.max).then_inc(max_done, 1)
                        dve.wait_ge(max_done, u + 1)
                        dve.wait_ge(exp_done, u + 1)
                        dve.tensor_tensor(diff[:, sl].rearrange("p (j b) k -> p b j k", b=2), s4,
                                          row_max[:, sl, :].rearrange("p (b j x) -> p b j x", b=2, x=1).broadcast_to([P, 2, 2, LOC_KEYS]),
                                          ALU.subtract).then_inc(diff_done, 1)
                    elif kind == "PV":
                        z = ps[:, Z_BANK, 0:GROUP * VW].rearrange("p (j d) -> p j d", d=VW)
                        dve.wait_ge(z_filled, 5 * n + g + 1)
                        dve.reciprocal(rden[:].rearrange("p (j x) -> p j x", x=1), z[:, :, LOC_HD:VW]).then_inc(rden_done, 1)
                        dve.wait_ge(rden_done, u + 1)
                        dve.tensor_tensor(zn[:, 4 * g:4 * g + 4, :], z[:, :, 0:LOC_HD],
                                          rden[:].rearrange("p (j x) -> p j x", x=1).broadcast_to([P, GROUP, LOC_HD]), ALU.mult).then_inc(zn_done, 1)
                        dve.wait_ge(zn_done, u + 9)
                        dve.sem_inc(z_free, 1)
                    elif kind == "WO":
                        dve.wait_ge(z_filled, 5 * n + 5)
                        dve.tensor_tensor(at(keep.y_mid, tile), ps[:, Z_BANK, 0:P], at(keep.y_in, tile), ALU.add).then_inc(mid_done, 1)
                        dve.wait_ge(mid_done, n + 1)
                        dve.sem_inc(z_free, 1)

                def ff(l, sa, sc, sd, par):
                    if sa is not None:
                        n = l * ALL_TILES + sa
                        dve.wait_ge(xn_done, n + 1)
                        dve.tensor_copy(xs[:, par, 0:HALF], at(keep.y_mid, sa)[:, 0:HALF]).then_inc(xs_half, 1)
                        dve.wait_ge(a_filled, n + 1)
                        dve.tensor_copy(xs[:, par, HALF:], ps[:, A_BANK, 0:HALF]).then_inc(xs_done, 1)
                        dve.wait_ge(xs_done, n + 2)
                        dve.wait_ge(xs_half, n + 1)
                        dve.bn_stats(stats[:], xs[:, par]).then_inc(stats_done, 1)
                        dve.wait_ge(stats_done, n + 1)
                        dve.nop(nofuse=True)
                        dve.bn_aggr(meanvar[:, par], stats[:]).then_inc(mv_done, 1)
                    if sc is not None:
                        n = l * ALL_TILES + sc
                        dve.wait_ge(h_filled, n + 1)
                        bias = b1[:, bass.ds(l & 1, 1)].rearrange("p a n -> p (a n)")
                        dve.wait_ge(prod_done, n + 1)
                        dve.tensor_tensor(gate[:, par], ps[:, H_BANK + 2 * par + 1, 0:DIM_INNER], bias[:, DIM_INNER:], ALU.add).then_inc(gate_done, 1)
                        dve.tensor_tensor(a_sb[:, par], ps[:, H_BANK + 2 * par, 0:DIM_INNER], bias[:, 0:DIM_INNER], ALU.add).then_inc(a_done, 1)
                    if sa is not None:
                        n = l * ALL_TILES + sa
                        dve.wait_ge(rstd_done, n + 1)
                        dve.tensor_scalar(xn[:, par], xs[:, par], meanvar[:, par, 0:1], rstd[:], ALU.subtract, ALU.mult).then_inc(xn_done, 1)
                    if sd is not None:
                        n = l * ALL_TILES + sd
                        dve.wait_ge(e_filled, n + 1)
                        dve.wait_ge(yb_done, n + 2)
                        dve.tensor_tensor(at(keep.y_in, sd), ps[:, E_BANK, 0:P], yb[:, par], ALU.add).then_inc(out_done, 1)

                with dve.Fori(0, DEPTH) as l:
                    dve.wait_ge(w_loaded, (l + 1) * 16 * W_DMAS)
                    attention_steps(dve, l, front, back, VECTOR_ORDER)
                    dve.wait_ge(mid_done, (l + 1) * ALL_TILES)
                    ff_steps(dve, l, ff)
                    dve.wait_ge(out_done, (l + 1) * ALL_TILES + 2)

            @block.scalar
            def _(act):
                act.wait_ge(consts, 1)
                act.sem_inc(xT_done, 2)
                act.sem_inc(val_done, 2)
                act.sem_inc(qkT_done, 6)
                act.sem_inc(exp_done, 2)
                act.sem_inc(t_free, 1)
                act.sem_inc(tailT_done, 2)

                def front(l, tile, par, k):
                    n = l * ALL_TILES + tile
                    bank = ps[:, F_BANK + k % 2, :]
                    act.wait_ge(f_filled[k % 2], operand_use(k, n, tile) + 1)
                    if k == 0:
                        act.copy(xT[par][:], bank[:, 0:P]).then_inc(xT_done, 1)
                        act.wait_ge(xT_done, n + 3)
                    elif k <= 4:
                        c = 4 * n + k - 1
                        act.wait_ge(sumsq_done, c + 1)
                        act.activation(square[:, k % 2], bank[:], ACT.Square).then_inc(squared, 1)
                        return
                    elif k <= 6:
                        if k == 5 and not (isinstance(tile, int) and tile == 0):
                            act.wait_ge(tail_done[1 - par], 16 * GROUP * (n >> 1) + 16 * GROUP * par)
                        act.copy(val[par][:, 8 * (k - 5):8 * (k - 4), 0:LOC_HD], bank[:].rearrange("p (h d) -> p h d", d=LOC_HD)).then_inc(val_done, 1)
                        act.wait_ge(val_done, 2 * n + k - 5 + 3)
                    else:
                        j = k - 7
                        src = bank[:].rearrange("p (h t) -> p h t", t=P)
                        if j % 2 == 0:
                            for half in range(2):
                                o = slice(64 * half, 64 * half + 64)
                                dst = qT[par][o].rearrange("p (c two) q -> p c two q", two=2)[:, 2 * j:2 * j + 4, half, :]
                                act.copy(dst, src[o]).then_inc(qkT_done, 1)
                        else:
                            act.copy(kT[par][:, 2 * (j - 1):2 * (j - 1) + 4, WINDOW:], src).then_inc(qkT_done, 1)
                        act.wait_ge(qkT_done, 6 * n + (2, 3, 5, 6)[j] + 6)
                    act.sem_inc(f_free[k % 2], 1)

                def back(l, tile, par, piece):
                    n = l * ALL_TILES + tile
                    kind, g = piece.rstrip("0123"), int(piece[-1]) if piece[-1].isdigit() else 0
                    u = 4 * n + g
                    sl = g % 2
                    if kind == "E":
                        act.wait_ge(diff_done, u + 9)
                        act.activation(prob_prev[:, sl], diff[0:WINDOW, sl, :, 0:WINDOW], ACT.Exp, scale=QK_SCALE).then_inc(prev_exp_done, 1)
                        act.activation(prob[:, sl], diff[:, sl, :, WINDOW:], ACT.Exp, scale=QK_SCALE).then_inc(exp_done, 1)
                    elif kind == "T":
                        act.wait_ge(t_filled, 6 * n + T_INDEX[piece] + 1)
                        act.wait_ge(zn_done, u + 7)
                        act.copy(tailT[:, sl], ps[:, S_BANK + 2 * sl, 2 * LOC_KEYS:2 * LOC_KEYS + WINDOW]).then_inc(tailT_done, 1)
                        act.copy(probT[:, sl], ps[:, T_BANK, :].rearrange("p (j q) -> p j q", q=P)).then_inc(t_free, 1)
                    elif kind == "TZ":
                        act.wait_ge(t_filled, 6 * n + T_INDEX[piece] + 1)
                        act.wait_ge(z_free, 5 * n + 1)
                        act.copy(znT[:, 4 * g:4 * g + 4, :], ps[:, T_BANK, :].rearrange("p (j q) -> p j q", q=P)).then_inc(znT_done, 1)
                        act.wait_ge(znT_done, 2 * n + g + 1)
                        act.sem_inc(t_free, 1)

                def ff(l, sa, sc, sd, par):
                    if sc is not None:
                        n = l * ALL_TILES + sc
                        act.wait_ge(b_filled, n + 1)
                        act.nop(nofuse=True)
                        act.activation(xnT[:, par], ps[:, B_BANK, 0:P], ACT.Identity, bias=ln[:, bass.ds(l, 1), 1:2].rearrange("p a b -> p (a b)"),
                                       scale=ln[:, bass.ds(l, 1), 0:1].rearrange("p a b -> p (a b)")).then_inc(xnT_done, 1)
                    if sd is not None:
                        n = l * ALL_TILES + sd
                        act.wait_ge(d_filled, n + 1)
                        act.copy(prodT[:, par, 0:2], ps[:, D_BANK, 0:2 * P].rearrange("p (c t) -> p c t", t=P))
                        act.copy(prodT[0:UC[2][1], par, 2], ps[0:UC[2][1], D_BANK, 2 * P:3 * P]).then_inc(prodT_done, 1)
                    if sc is not None:
                        n = l * ALL_TILES + sc
                        act.wait_ge(gate_done, n + 1)
                        act.activation(gelu[:, par], gate[:, par], ACT.Gelu).then_inc(gelu_done, 1)

                with act.Fori(0, DEPTH) as l:
                    attention_steps(act, l, front, back)
                    act.wait_ge(mid_done, (l + 1) * ALL_TILES)
                    ff_steps(act, l, ff)
                    act.wait_ge(out_done, (l + 1) * ALL_TILES + 2)


def output_phase(nc, keep, parked, out):
    with ExitStack() as ctx:
        m = Mem(nc, ctx)
        x = m.sb("out_x", [P, ALL_TILES, P])
        summed, stored = m.sem("summed"), m.sem("stored")
        fetched = [m.sem(f"fetched{b}") for b in range(BATCH)]
        with nc.Block() as block:

            @block.vector
            def _(dve):
                for b in range(BATCH):
                    row = x[:, b * TILES:(b + 1) * TILES, :]
                    first = b * (TILES + 1) + 1
                    dve.wait_ge(fetched[b], 16)
                    dve.tensor_tensor(row, row, keep.y_in[:, first:first + TILES, :], ALU.add).then_inc(summed, 1)

            @block.sync
            def _(sp):
                for b in range(BATCH):
                    part = slice(b * TILES, (b + 1) * TILES)
                    sp.dma_start(x[:, part, :], parked[:, part, :]).then_inc(fetched[b], 16)
                for b in range(BATCH):
                    sp.wait_ge(summed, b + 1)
                    sp.dma_start(out.rearrange("b (t p) c -> p b t c", p=P)[:, b], x[:, b * TILES:(b + 1) * TILES, :]).then_inc(stored, 16)
                sp.wait_ge(stored, 16 * BATCH)


def rotary_angles(n, hd, np):
    half = np.arange(0, hd, 2, dtype=np.float32)
    inv = (1.0 / np.power(np.float32(10000.0), half / np.float32(hd))).astype(np.float32)
    f = np.arange(n, dtype=np.float32)[:, None] * inv[None, :]
    return np.concatenate([f, f], -1), half


def shape_tables(np):
    t = {}
    by_tile = lambda a: np.ascontiguousarray(a.reshape(TILES, P, -1).transpose(1, 0, 2))
    f, _ = rotary_angles(SEQ, L1_HD, np)
    sign = np.where(np.arange(L1_HD) < L1_HD // 2, -1.0, 1.0).astype(np.float32)
    t["l1_cos"], t["l1_sin"] = by_tile(np.cos(f)), by_tile(np.sin(f) * sign)
    f, half = rotary_angles(SEQ, LOC_HD, np)
    base = (half + np.float32(0.4 * LOC_HD)) / np.float32(1.4 * LOC_HD)
    power = (np.arange(SEQ, dtype=np.float32) - SEQ // 2) / np.float32(WINDOW // 2)
    scale = np.power(base[None, :], power[:, None]).astype(np.float32)
    scale = np.concatenate([scale, scale], -1)
    inv = (np.float32(1.0) / scale).astype(np.float32)
    sign = np.where(np.arange(LOC_HD) < LOC_HD // 2, -1.0, 1.0).astype(np.float32)
    c, s = np.cos(f), np.sin(f) * sign
    t["lo_rotary"] = np.stack([by_tile(x) for x in (c * scale, s * scale, c * inv, s * inv)], 1)
    i = np.arange(P)[:, None]
    t["mask0"] = np.where(np.arange(P)[None, :] > i, L0_MASK, 0.0)
    j = np.arange(LOC_KEYS)[None, :] - WINDOW
    hidden = (j > i) | (j < i - WINDOW)
    mask = np.stack([hidden | (j < 0)] + [hidden] * (TILES - 1), 1)
    t["lo_mask"] = np.where(mask, -1e30, 0.0)
    t["lo_shift"] = np.stack([np.eye(P, k=1), np.eye(P, k=1 - P)], 1)
    t["ident"] = np.eye(P)
    t = {k: np.ascontiguousarray(v, dtype=np.float32) for k, v in t.items()}
    for k in ("mask0", "lo_mask"):
        t[k] = t[k].astype(mybir.dt.np(BF16))
    return t


def kernel(**x):
    import numpy as np
    import concourse.bacc as bacc
    from concourse.bass_utils import run_bass_kernel_spmd

    x = {k: np.asarray(v) for k, v in x.items()}
    flat = lambda w: w.reshape(HEADS * L0_HD, DIM).T
    arrays = {
        "x": x["L0_attn_x"].reshape(BATCH * SEQ, DIM),
        "l0_w": np.stack([flat(x["L0_attn_W_K"]), flat(x["L0_attn_W_Q"]), flat(x["L0_attn_W_V"])]),
        "l0_wo": x["L0_attn_W_O"].transpose(0, 2, 1).reshape(HEADS * L0_HD, DIM),
        "w8T": x["L0_ffn_weight"].T, "bias0": x["L0_ffn_bias"],
        "l1_w": x["L1_attn_w_qkv"].T, "l1_wo": x["L1_attn_w_out"].T, "b_out": x["L1_attn_b_out"],
        "Wqkv": x["L1_ffn_Wqkv"], "Wo": x["L1_ffn_Wo"], "W1": x["L1_ffn_W1"], "W2": x["L1_ffn_W2"],
        "b1": x["L1_ffn_b1"], "b2": x["L1_ffn_b2"],
        "ln": np.stack([x["L1_ffn_ln_g"].T, x["L1_ffn_ln_b"].T], -1),
    }
    q, k = x["L1_ffn_q_scale"], x["L1_ffn_k_scale"]
    swap = lambda s: np.concatenate([s[:, LOC_HD // 2:], s[:, :LOC_HD // 2]], -1)
    arrays["lo_scales"] = np.stack([q, swap(q), k, swap(k)], 1)
    arrays.update(shape_tables(np))
    nc = bacc.Bacc("TRN2", target_bir_lowering=False, num_devices=1)
    dram = {}
    for name, value in arrays.items():
        arrays[name] = np.ascontiguousarray(value)
        dram[name] = nc.dram_tensor(f"in_{name}", arrays[name].shape, mybir.dt.from_np(arrays[name].dtype), kind="ExternalInput").ap()
    out = nc.dram_tensor("out", (BATCH, SEQ, DIM), F32, kind="ExternalOutput").ap()
    build(nc, dram, out)
    r = run_bass_kernel_spmd(nc, [{f"in_{k}": v for k, v in arrays.items()}], core_ids=[0])
    return r.results[0]["out"]
```
